# Optimizing a Trainium2 kernel written in Bass

```python
import numpy as np
import jax
import jax.numpy as jnp

def _softmax(x, axis=-1):
    return jax.nn.softmax(x, axis=axis)

def _gelu(x):
    return jax.nn.gelu(x, approximate=True)

def _silu(x):
    return jax.nn.silu(x)

def _sigmoid(x):
    return jax.nn.sigmoid(x)

def _layernorm(x, axis=-1, eps=1e-05):
    m = jnp.mean(x, axis=axis, keepdims=True)
    v = jnp.var(x, axis=axis, keepdims=True)
    return (x - m) / jnp.sqrt(v + eps)

def _scatter_add(tgt, idx, src, axis=0):
    return tgt.at[idx].add(src)

def _segment_sum(src, seg, n):
    return jax.ops.segment_sum(src, seg, n)
kernel_name = 'mk_gnn_ffn_d1_gnn_r8_ee8157'

def setup_inputs(seed: int=0):
    np.random.seed(seed)
    _w = jnp.asarray

    def _rec_inputs():
        import jax
        import jax.numpy as jnp
        _gk = jax.random.key(seed)
        x = -0.0002117 + 1 * jax.random.normal(jax.random.fold_in(_gk, 1), (6250, 256), jnp.float32)
        _s = jax.random.randint(jax.random.fold_in(_gk, 2), (100000,), 0, 6250, jnp.int32)
        _d = jax.random.randint(jax.random.fold_in(_gk, 3), (100000,), 0, 6250, jnp.int32)
        _loop = jnp.arange(6250, dtype=jnp.int32)
        src = jnp.concatenate([_s, _d, _loop])
        dst = jnp.concatenate([_d, _s, _loop])
        _o = jnp.argsort(dst, stable=True)
        src = src[_o]
        dst = dst[_o]
        return (x, src, dst)
    x, src, dst = _rec_inputs()

    def _L0_gnn_setup():
        import jax, jax.numpy as jnp
        import numpy as np
        N = 12500
        D = 256
        E = 400000
        key = jax.random.key(seed)
        ks = jax.random.split(key, 8)
        x = jax.random.normal(ks[0], (N, D), dtype=jnp.float32)
        edge_index = jax.random.randint(ks[1], (2, E), 0, N, dtype=jnp.int64)
        s = 1.0 / np.sqrt(D)
        W_l = jax.random.uniform(ks[2], (D, D), dtype=jnp.float32, minval=-s, maxval=s)
        b_l = jax.random.uniform(ks[3], (D,), dtype=jnp.float32, minval=-s, maxval=s)
        W_r = jax.random.uniform(ks[4], (D, D), dtype=jnp.float32, minval=-s, maxval=s)
        ln_gamma = jnp.ones((D,), dtype=jnp.float32)
        ln_beta = jnp.zeros((D,), dtype=jnp.float32)
        return {'x': x, 'edge_index': edge_index, 'W_l': W_l, 'b_l': b_l, 'W_r': W_r, 'ln_gamma': ln_gamma, 'ln_beta': ln_beta}
    _L0_gnn_all = _L0_gnn_setup()
    _L0_gnn_in = {k: v for k, v in _L0_gnn_all.items() if k in ('W_l', 'b_l', 'W_r', 'ln_gamma', 'ln_beta')}
    del _L0_gnn_all

    def _L0_ffn_setup():
        import jax, jax.numpy as jnp
        import numpy as np
        B, S, H, F, E, K = (8, 512, 256, 512, 16, 2)
        EPS = 1e-05
        key = jax.random.key(seed)
        ks = jax.random.split(key, 9)
        sc = 0.02
        return {'x': jax.random.normal(ks[0], (B, S, H), dtype=jnp.float32), 'gate_w': jax.random.normal(ks[1], (H, E), dtype=jnp.float32) * sc, 'gate_b': jnp.zeros((E,), dtype=jnp.float32), 'w1': jax.random.normal(ks[2], (E, H, F), dtype=jnp.float32) * sc, 'b1': jnp.zeros((E, F), dtype=jnp.float32), 'w2': jax.random.normal(ks[3], (E, F, H), dtype=jnp.float32) * sc, 'b2': jnp.zeros((E, H), dtype=jnp.float32), 'gamma': jnp.ones((H,), dtype=jnp.float32), 'beta': jnp.zeros((H,), dtype=jnp.float32)}
    _L0_ffn_all = _L0_ffn_setup()
    _L0_ffn_in = {k: v for k, v in _L0_ffn_all.items() if k in ('gate_w', 'gate_b', 'w1', 'b1', 'w2', 'b2', 'gamma', 'beta')}
    del _L0_ffn_all
    return {'x': x, 'src': src, 'dst': dst, 'L0_gnn_W_l': _L0_gnn_in['W_l'], 'L0_gnn_b_l': _L0_gnn_in['b_l'], 'L0_gnn_W_r': _L0_gnn_in['W_r'], 'L0_gnn_ln_gamma': _L0_gnn_in['ln_gamma'], 'L0_gnn_ln_beta': _L0_gnn_in['ln_beta'], 'L0_ffn_gate_w': _L0_ffn_in['gate_w'], 'L0_ffn_gate_b': _L0_ffn_in['gate_b'], 'L0_ffn_w1': _L0_ffn_in['w1'], 'L0_ffn_b1': _L0_ffn_in['b1'], 'L0_ffn_w2': _L0_ffn_in['w2'], 'L0_ffn_b2': _L0_ffn_in['b2'], 'L0_ffn_gamma': _L0_ffn_in['gamma'], 'L0_ffn_beta': _L0_ffn_in['beta']}

def reference(x, src, dst, L0_gnn_W_l, L0_gnn_b_l, L0_gnn_W_r, L0_gnn_ln_gamma, L0_gnn_ln_beta, L0_ffn_gate_w, L0_ffn_gate_b, L0_ffn_w1, L0_ffn_b1, L0_ffn_w2, L0_ffn_b2, L0_ffn_gamma, L0_ffn_beta):
    import jax
    import jax.numpy as jnp

    def _L0_gnn_ref(x, edge_index, W_l, b_l, W_r, ln_gamma, ln_beta):
        import jax, jax.numpy as jnp
        import numpy as np
        N = 12500
        D = 256
        E = 400000
        src, dst = (edge_index[0], edge_index[1])
        n = x.shape[0]
        msg_sum = jax.ops.segment_sum(x[src], dst, num_segments=n)
        deg = jax.ops.segment_sum(jnp.ones((src.shape[0],), x.dtype), dst, num_segments=n)
        agg = msg_sum / jnp.maximum(deg, 1.0)[:, None]
        f = agg @ W_l.T + b_l + x @ W_r.T
        f = jax.nn.gelu(f, approximate=False)
        mu = jnp.mean(f, axis=-1, keepdims=True)
        var = jnp.var(f, axis=-1, keepdims=True)
        f = (f - mu) * jax.lax.rsqrt(var + 1e-05) * ln_gamma + ln_beta
        return f + x

    def _L0_ffn_ref(x, gate_w, gate_b, w1, b1, w2, b2, gamma, beta):
        import jax, jax.numpy as jnp
        import numpy as np
        B, S, H, F, E, K = (8, 512, 256, 512, 16, 2)
        EPS = 1e-05
        gate_logits = x @ gate_w + gate_b
        topk_vals, topk_idx = jax.lax.top_k(gate_logits, K)
        topk_w = jax.nn.softmax(topk_vals, axis=-1)
        h = jax.nn.relu(jnp.einsum('bsh,ehf->bsef', x, w1) + b1)
        expert_out = jnp.einsum('bsef,efh->bseh', h, w2) + b2
        sel = jnp.take_along_axis(expert_out, topk_idx[:, :, :, None], axis=2)
        moe = jnp.sum(topk_w[..., None] * sel, axis=2)
        y = x + moe
        mu = jnp.mean(y, axis=-1, keepdims=True)
        var = jnp.var(y, axis=-1, keepdims=True)
        return (y - mu) / jnp.sqrt(var + EPS) * gamma + beta
    edge_index = jnp.stack([src, dst])
    x = x + _L0_gnn_ref(_layernorm(x, axis=-1), edge_index, L0_gnn_W_l, L0_gnn_b_l, L0_gnn_W_r, L0_gnn_ln_gamma, L0_gnn_ln_beta)
    x = x + _L0_ffn_ref(_layernorm(x, axis=-1)[None], L0_ffn_gate_w, L0_ffn_gate_b, L0_ffn_w1, L0_ffn_b1, L0_ffn_w2, L0_ffn_b2, L0_ffn_gamma, L0_ffn_beta)[0]
    return x

_drawn_inputs = setup_inputs


def setup_inputs(seed=0):
    import zlib

    import numpy as np

    out = dict(_drawn_inputs(seed))
    spreads = {'L0_gnn_ln_gamma': (1.0, 0.2),
     'L0_gnn_ln_beta': (0.0, 0.1),
     'L0_ffn_gate_b': (0.0, 0.375),
     'L0_ffn_b1': (0.0, 0.8),
     'L0_ffn_b2': (0.0, 0.352),
     'L0_ffn_gamma': (1.0, 0.2),
     'L0_ffn_beta': (0.0, 0.1)}
    factors = {'L0_ffn_w1': 2.961}
    for name, (base, spread) in spreads.items():
        noise = np.random.default_rng([zlib.crc32(name.encode()), seed]).standard_normal(out[name].shape)
        drawn = base * np.exp(spread * noise) if base else spread * noise
        out[name] = jnp.asarray(drawn.astype(out[name].dtype))
    for name, factor in factors.items():
        out[name] = (out[name] * factor).astype(out[name].dtype)
    return out
```

```python
from contextlib import ExitStack

import concourse.bass as bass
from concourse import mybir

F32 = mybir.dt.float32
I32 = mybir.dt.int32
ALU = mybir.AluOpType
ACT = mybir.ActivationFunctionType
AX = mybir.AxisListType

P = 128
EPS = 1e-5


class Tile:

    def __init__(self, i, c):
        self.i, self.c = i, c
        self.slot = c % 2
        self.n = i * 2 + c if not isinstance(i, int) else 2 * i + c
        self.round = i + c // 2

    def __add__(self, k):
        return Tile(self.i, self.c + k)

    def inside(self, total):
        return not isinstance(self.i, int) or 0 <= self.n < total


def pipelined(eng, total, before, after, step):
    first = after + after % 2
    rounds = (total - before - first) // 2
    for n in range(-before, first):
        step(Tile(0, n))
    with eng.Fori(0, rounds) as i:
        step(Tile(i, first))
        step(Tile(i, first + 1))
    for n in range(first + 2 * rounds, total + after):
        step(Tile(0, n))


def build(nc, x, edges, heads, w_l, w_r, b_l, gamma1, beta1, gate_w, gate_b, w1, b1, w2, b2,
          gamma2, beta2, out):
    NODES, D = out.shape
    T = x.shape[0] // P
    CHUNKS = edges.shape[0]
    NODE_TILES = -(-(NODES + 1) // P)
    E, _, F = w1.shape
    KD, KF = D // P, F // P
    NI = -(-(CHUNKS + NODE_TILES - 1) // 16) * 16
    IC = NI // P
    assert NI % P == 0 and T % 10 == 0 and NODE_TILES <= T
    MT = -(-((2 * T * P + E * (P - 1)) // P) // 2) * 2
    DA = D + 1
    RS = D + 4

    xn_d = nc.dram_tensor("xn_d", [T * P, D], F32).ap()
    xn2_d = nc.dram_tensor("xn2_d", [T * P, D], F32).ap()
    x1_d = nc.dram_tensor("x1_d", [T * P, D], F32).ap()
    xs_d = nc.dram_tensor("xs_d", [MT * P, D], F32).ap()
    ys_d = nc.dram_tensor("ys_d", [MT * P, D], F32).ap()
    tt_d = nc.dram_tensor("tt_d", [IC, P], I32).ap()

    with ExitStack() as ctx:
        def sb(name, cols, dt=F32):
            return ctx.enter_context(nc.sbuf_tensor(name, [P, cols], dt))

        def sem(name):
            return ctx.enter_context(nc.semaphore(name))

        bank = [ctx.enter_context(nc.psum_tensor(f"bank{i}", [P, 512], F32)) for i in range(8)]

        W1N, W2N = E * KD * F, E * KF * D
        big = sb("big", W1N + W2N)
        w1_sb = big[:, 0:W1N]
        w2_sb = big[:, W1N:W1N + W2N]
        acc = sb("acc", T * DA)
        acc3 = acc[:, :].rearrange("p (t d) -> p t d", d=DA)

        cursor = [0]

        def part(base, cols):
            at = base + cursor[0]
            cursor[0] += cols
            assert cursor[0] <= W1N
            return big[:, at:at + cols]

        xn = part(0, T * D)
        tile_of_item = part(0, NI).bitcast(I32)
        cursor[0] = 0
        item_src = part(W1N, NI).bitcast(I32)
        item_dst = part(W1N, NI + 8)
        kept = cursor[0]
        pairs_i = part(W1N, IC * 2 * P).bitcast(I32)
        pairs_f = part(W1N, IC * 2 * P)
        head_i = part(W1N, CHUNKS).bitcast(I32)
        chunk_no = part(W1N, CHUNKS)
        starts = part(W1N, CHUNKS)
        junk = pairs_f[:, 0:CHUNKS]
        cursor[0] = kept
        rows = part(W1N, 16 * RS)
        onehot = part(W1N, 16 * P)
        cursor[0] = 0
        wl_sb = part(W1N, KD * D)
        wr_sb = part(W1N, KD * D)
        bl_sb = part(W1N, D)
        g1_sb = part(W1N, D)
        be1_sb = part(W1N, D)
        gw_sb = part(W1N, KD * E)
        gb_sb = part(W1N, E)
        logits = part(W1N, T * E)
        kept = cursor[0]
        agg_s = [part(W1N, D) for _ in range(2)]
        xn_s = [part(W1N, D) for _ in range(2)]
        aggx_t = [part(W1N, 2 * D) for _ in range(2)]
        x_s = [part(W1N, D) for _ in range(2)]
        xs_s = [part(W1N, D) for _ in range(2)]
        u_s = [part(W1N, D) for _ in range(2)]
        ug_s = [part(W1N, D) for _ in range(2)]
        xn2_s = [part(W1N, D) for _ in range(2)]
        xn2_t = [part(W1N, D) for _ in range(2)]
        cursor[0] = kept
        TE = T * E
        eq, cand, oh1, oh2, lg2, both, cum, tot, inc, pos_all, prod = [part(W1N, TE) for _ in range(11)]
        cmp_ = part(W1N, MT * E)
        b2_sb = acc[:, 0:E * D]
        at = [E * D]

        def work(cols):
            at[0] += cols
            return acc[:, at[0] - cols:at[0]]

        sc_rows = [work(D) for _ in range(5)]
        xi = [work(D) for _ in range(2)]
        xi_t = [work(D) for _ in range(2)]
        h_sb = [work(F) for _ in range(2)]
        h_t = [work(F) for _ in range(2)]
        y_sb = [work(D) for _ in range(2)]
        cursor[0] = 0
        d_x = [part(0, D) for _ in range(5)]
        d_y1 = [part(0, D) for _ in range(5)]
        d_y2 = [part(0, D) for _ in range(5)]
        d_t = [part(0, D) for _ in range(5)]
        o_t = [part(0, D) for _ in range(5)]
        d_o = [part(0, D) for _ in range(5)]

        ident = sb("ident", P)
        iota = sb("iota", P)
        below = sb("below", P)
        ones = sb("ones", P)
        zeros = sb("zeros", D)
        g2_sb = sb("g2_sb", D)
        be2_sb = sb("be2_sb", D)
        b1_sb = sb("b1_sb", E * KF)
        stats = sb("stats", T * 6)
        st = {n: sb(f"st_{n}", T) for n in ("sum", "dif", "var", "std", "mean", "rstd", "nmr")}
        rdeg = sb("rdeg", T)
        item_no = sb("item_no", IC)
        item_c = sb("item_c", IC)
        item_ci = sb("item_ci", IC, I32)
        item_t = sb("item_t", IC)
        item_nt = sb("item_nt", IC)
        item_tc = sb("item_tc", IC)
        item_ti = sb("item_ti", P, I32)
        src_stage = sb("src_stage", 16, I32)
        e_no = sb("e_no", E)
        m_no = sb("m_no", MT)
        v1, v2, i1, i2, p1, p2, ed = [sb(n, T) for n in ("v1", "v2", "i1", "i2", "p1", "p2", "ed")]
        posf = sb("posf", 2 * T)
        pos_i = sb("pos_i", 2 * T, I32)
        pos_stage = sb("pos_stage", 10, I32)
        nt_i = sb("nt_i", E, I32)
        nt_f = sb("nt_f", E)
        end_f = sb("end_f", E)
        base_f = sb("base_f", E)
        et_f = sb("et_f", MT)
        et_i = sb("et_i", MT, I32)

        turns = sem("turns")
        stage = [sem(f"stage{i}_done") for i in range(9)]
        heads_in, params_in, late_in = sem("heads_in"), sem("params_in"), sem("late_in")
        x_in = [sem(f"x_in{i}") for i in range(5)]
        consts_ready, masks_ready, acc_zero = sem("consts_ready"), sem("masks_ready"), sem("acc_zero")
        chunk_ready, nt_ready = sem("chunk_ready"), sem("nt_ready")
        pairs_in, pairs_ready, tables_t = sem("pairs_in"), sem("pairs_ready"), sem("tables_t")
        tc_ready, ti_ready, ti_out, ti_in = sem("tc_ready"), sem("ti_ready"), sem("ti_out"), sem("ti_in")
        var_ready = [sem(f"var{i}_ready") for i in range(4)]
        std_ready = [sem(f"std{i}_ready") for i in range(4)]
        norm_ready = [sem(f"norm{i}_ready") for i in range(4)]
        xn_even, xn_odd, xn_out = sem("xn_even"), sem("xn_odd"), sem("xn_out")
        idx_ready, oh_ready, mm_done, acc_done = sem("idx_ready"), sem("oh_ready"), sem("mm_done"), sem("acc_done")
        rows_in = [sem(f"rows_in{k}") for k in range(16)]
        agg_ready, xns_ready, tr_done, tt_ready = sem("agg_ready"), sem("xns_ready"), sem("tr_done"), sem("tt_ready")
        f_done, gelu_done, xs0_out = sem("f_done"), sem("gelu_done"), sem("xs0_out")
        xt_in = [sem(f"xt_in{k}") for k in range(2)]
        u_ready, s1_ready, xs_ready, ug_ready, x1_ready = sem("u_ready"), sem("s1_ready"), sem("xs_ready"), sem("ug_ready"), sem("x1_ready")
        x1_out, w1_in, w2_in, b2_in = sem("x1_out"), sem("w1_in"), sem("w2_in"), sem("b2_in")
        xn2_ready, tr2_done, t2_ready, lg_done, lg_ready = sem("xn2_ready"), sem("tr2_done"), sem("t2_ready"), sem("lg_done"), sem("lg_ready")
        xn2_out = [sem(f"xn2_out{k}") for k in range(2)]
        diff_ready, exp_ready, both_ready, counts_done = sem("diff_ready"), sem("exp_ready"), sem("both_ready"), sem("counts_done")
        sc_in = [sem(f"sc_in{k}") for k in range(5)]
        sc_out = [sem(f"sc_out{k}") for k in range(5)]
        pos_ready, pos_used = sem("pos_ready"), sem("pos_used")
        xi_in = [sem(f"xi_in{k}") for k in range(2)]
        y_out = [sem(f"y_out{k}") for k in range(2)]
        xt_done, xit_ready, mm1_done, h_ready = sem("xt_done"), sem("xit_ready"), sem("mm1_done"), sem("h_ready")
        ht_done, ht_ready, mm2_done, y_ready = sem("ht_done"), sem("ht_ready"), sem("mm2_done"), sem("y_ready")
        d_in = [sem(f"d_in{k}") for k in range(5)]
        dy_in = [sem(f"dy_in{k}") for k in range(5)]
        dpos_ready, d_done = sem("dpos_ready"), sem("d_done")
        o_in = [sem(f"o_in{k}") for k in range(5)]
        o_out = [sem(f"o_out{k}") for k in range(5)]
        yn_ready, o_ready = sem("yn_ready"), sem("o_ready")

        block = ctx.enter_context(nc.Block())

        def turn(eng, s, value):
            eng.wait_ge(s, value)
            if not isinstance(value, int):
                eng.sem_inc(turns, 1)

        def stage_end(eng, k):
            eng.drain().then_inc(stage[k], 1)
            eng.wait_ge(stage[k], 5)

        def cols(t, n, width):
            return t[:, bass.ds(n * width, width)] if not isinstance(n, int) else t[:, n * width:(n + 1) * width]

        def acc_cols(n, w=D):
            return acc[:, bass.ds(n * DA, w)] if not isinstance(n, int) else acc[:, n * DA:n * DA + w]

        def dram_rows(t, n, count=P):
            return t[bass.ds(n * P, count), :] if not isinstance(n, int) else t[n * P:n * P + count, :]

        def w1_view():
            return w1_sb.rearrange("p (e k f) -> p e k f", e=E, k=KD), w1.rearrange("e (k p) f -> p e k f", p=P)

        def w2_view():
            return w2_sb.rearrange("p (e k h) -> p e k h", e=E, k=KF), w2.rearrange("e (k p) h -> p e k h", p=P)

        @block.sync
        def _(sp):
            sp.dma_start(head_i, heads.to_broadcast([P, CHUNKS])).then_inc(heads_in, 16)
            for c in range(5):
                n = T // 5
                sp.dma_start(xn[:, c * n * D:(c + 1) * n * D].rearrange("p (t d) -> p t d", d=D),
                             x[c * n * P:(c + 1) * n * P, :].rearrange("(t p) d -> p t d", p=P)).then_inc(x_in[c], 16)
            sp.dma_start(g2_sb[:, :], gamma2.to_broadcast([P, D])).then_inc(params_in, 16)
            sp.dma_start(be2_sb[:, :], beta2.to_broadcast([P, D])).then_inc(params_in, 16)
            sp.dma_start(b1_sb[:, :], b1).then_inc(params_in, 16)
            sp.wait_ge(ti_ready, 1)
            sp.dma_start(tt_d, item_ti[0:IC, :]).then_inc(ti_out, 16)
            sp.wait_ge(ti_out, 16)
            sp.dma_start(tile_of_item[0:1, :], tt_d.rearrange("(a j) p -> a (j p)", a=1)).then_inc(ti_in, 16)
            for c in range(5):
                n = T // 5
                sp.wait_ge(xn_even, n // 2 * (c + 1))
                sp.wait_ge(xn_odd, n // 2 * (c + 1))
                sp.dma_start(xn_d[c * n * P:(c + 1) * n * P, :].rearrange("(t p) d -> p t d", p=P),
                             xn[:, c * n * D:(c + 1) * n * D].rearrange("p (t d) -> p t d", d=D)).then_inc(xn_out, 16)
            sp.wait_ge(xn_out, 16 * 5)
            sp.wait_ge(ti_in, 16)
            sp.wait_ge(params_in, 16 * 3)
            stage_end(sp, 0)

            sp.dma_start(xs_d.rearrange("(p m) d -> p m d", p=P),
                         zeros[:, :].rearrange("p (a d) -> p a d", a=1).to_broadcast([P, MT, D])).then_inc(xs0_out, 16)
            stage_end(sp, 1)

            sp.dma_start(wl_sb.rearrange("p (k n) -> p k n", k=KD), w_l.rearrange("(k p) n -> p k n", p=P)).then_inc(late_in, 16)
            sp.dma_start(wr_sb.rearrange("p (k n) -> p k n", k=KD), w_r.rearrange("(k p) n -> p k n", p=P)).then_inc(late_in, 16)
            sp.dma_start(bl_sb[0:1, :], b_l).then_inc(late_in, 16)
            sp.dma_start(g1_sb, gamma1.to_broadcast([P, D])).then_inc(late_in, 16)
            sp.dma_start(be1_sb, beta1.to_broadcast([P, D])).then_inc(late_in, 16)
            sp.dma_start(gw_sb.rearrange("p (k n) -> p k n", k=KD), gate_w.rearrange("(k p) n -> p k n", p=P)).then_inc(late_in, 16)
            sp.dma_start(gb_sb[0:1, :], gate_b).then_inc(late_in, 16)
            stage_end(sp, 2)

            for n in range(2):
                sp.dma_start(x_s[n], dram_rows(x, n)).then_inc(xt_in[n], 16)
            with sp.Fori(0, T // 2 - 1) as i:
                for k in range(2):
                    turn(sp, s1_ready, 2 * i + k + 1)
                    sp.dma_start(x_s[k], dram_rows(x, 2 * i + k + 2)).then_inc(xt_in[k], 16)
            stage_end(sp, 3)

            sp.dma_start(x1_d.rearrange("(t p) d -> p t d", p=P), acc3[:, :, 0:D]).then_inc(x1_out, 16)
            w1_dst, w1_src = w1_view()
            for e in range(E):
                sp.dma_start(w1_dst[:, e], w1_src[:, e]).then_inc(w1_in, 16)
            with sp.Fori(0, T // 2) as i:
                for k in range(2):
                    turn(sp, xn2_ready, 2 * i + k + 3)
                    sp.dma_start(dram_rows(xn2_d, 2 * i + k), xn2_s[k]).then_inc(xn2_out[k], 16)
            for k in range(2):
                sp.wait_ge(xn2_out[k], 16 * (T // 2 + 1))
            sp.wait_ge(x1_out, 16)
            sp.wait_ge(xs0_out, 16)
            stage_end(sp, 4)
            stage_end(sp, 5)

            sp.dma_start(b2_sb, b2.to_broadcast([P, E * D])).then_inc(b2_in, 16)
            for k in range(5):
                sp.dma_start(sc_rows[k], dram_rows(xn2_d, k)).then_inc(sc_in[k], 16)
            w2_dst, w2_src = w2_view()
            for e in range(E):
                sp.dma_start(w2_dst[:, e], w2_src[:, e]).then_inc(w2_in, 16)
            with sp.Fori(0, T // 5 - 1) as i:
                for k in range(5):
                    turn(sp, sc_out[k], 32 * i + 32)
                    sp.dma_start(sc_rows[k], dram_rows(xn2_d, 5 * i + k + 5)).then_inc(sc_in[k], 16)
            sp.wait_ge(b2_in, 16)
            sp.wait_ge(w1_in, 16 * E)
            sp.wait_ge(w2_in, 16 * E)
            for k in range(5):
                sp.wait_ge(sc_out[k], 32 * (T // 5))
            stage_end(sp, 6)

            def load_rows(n, slot):
                turn(sp, xt_done, n - 1)
                sp.dma_start(xi[slot], dram_rows(xs_d, n)).then_inc(xi_in[slot], 16)

            def store_result(n, slot):
                turn(sp, y_ready, n + 3)
                sp.dma_start(dram_rows(ys_d, n), y_sb[slot]).then_inc(y_out[slot], 16)

            for n in range(2):
                sp.dma_start(xi[n], dram_rows(xs_d, n)).then_inc(xi_in[n], 16)
            load_rows(2, 0)
            with sp.Fori(0, MT // 2 - 2) as i:
                for k in range(2):
                    load_rows(2 * i + k + 3, 1 - k)
                    store_result(2 * i + k, k)
            load_rows(MT - 1, 1)
            for n in range(MT - 4, MT):
                store_result(n, n % 2)
            for k in range(2):
                sp.wait_ge(y_out[k], 16 * (MT // 2 + 1))
            stage_end(sp, 7)

            for k in range(5):
                sp.dma_start(d_x[k], dram_rows(xn2_d, k)).then_inc(d_in[k], 16)
            with sp.Fori(0, T // 5 - 1) as i:
                for k in range(5):
                    turn(sp, d_done, 5 * i + k + 1)
                    sp.dma_start(d_x[k], dram_rows(xn2_d, 5 * i + k + 5)).then_inc(d_in[k], 16)
            for k in range(5):
                sp.dma_start(o_t[k], dram_rows(x1_d, k)).then_inc(o_in[k], 16)
            full = NODES // P // 5 * 5
            assert full == T - 5
            with sp.Fori(0, full // 5) as i:
                for k in range(5):
                    turn(sp, o_ready, 5 * i + k + 1)
                    sp.dma_start(dram_rows(out, 5 * i + k), d_o[k]).then_inc(o_out[k], 16)
                    sp.dma_start(o_t[k], dram_rows(x1_d, 5 * i + k + 5)).then_inc(o_in[k], 16)
            for k in range(5):
                n = min(P, NODES - (full + k) * P)
                sp.wait_ge(o_ready, full + k + 1)
                if n > 0:
                    sp.dma_start(out[(full + k) * P:(full + k) * P + n, :], d_o[k][0:n, :]).then_inc(o_out[k], 16)
            for k in range(5):
                sp.wait_ge(o_out[k], 16 * (full // 5 + 1 + (NODES > (full + k) * P)))
            stage_end(sp, 8)

        @block.gpsimd
        def _(pool):
            pool.iota(chunk_no, pattern=[[1, CHUNKS]], base=0, channel_multiplier=0, allow_small_or_imprecise_dtypes=True).then_inc(consts_ready, 1)
            pool.iota(item_no[:, :], pattern=[[P, IC]], base=0, channel_multiplier=1, allow_small_or_imprecise_dtypes=True).then_inc(consts_ready, 1)
            pool.iota(iota[:, :], pattern=[[1, P]], base=0, channel_multiplier=0, allow_small_or_imprecise_dtypes=True).then_inc(consts_ready, 1)
            pool.iota(e_no[:, :], pattern=[[1, E]], base=0, channel_multiplier=0, allow_small_or_imprecise_dtypes=True).then_inc(consts_ready, 1)
            pool.iota(m_no[:, :], pattern=[[1, MT]], base=0, channel_multiplier=0, allow_small_or_imprecise_dtypes=True).then_inc(consts_ready, 1)
            pool.memset(ident[:, :], 0.0).then_inc(consts_ready, 1)
            pool.memset(below[:, :], 1.0).then_inc(consts_ready, 1)
            pool.memset(ones[:, :], 1.0).then_inc(consts_ready, 1)
            pool.memset(zeros[:, :], 0.0).then_inc(consts_ready, 1)
            pool.wait_ge(consts_ready, 9)
            pool.affine_select(out=ident[:, :], in_=ident[:, :], compare_op=ALU.not_equal, fill=1.0, base=0,
                               pattern=[[-1, P]], channel_multiplier=1).then_inc(masks_ready, 1)
            pool.affine_select(out=below[:, :], in_=below[:, :], compare_op=ALU.is_gt, fill=0.0, base=0,
                               pattern=[[1, P]], channel_multiplier=-1).then_inc(masks_ready, 1)
            pool.memset(acc[:, :], 0.0).then_inc(acc_zero, 1)
            pool.wait_ge(chunk_ready, 1)
            for j in range(IC):
                pool.indirect_dma_start(pairs_i[:, j * 2 * P:(j + 1) * 2 * P], None, edges,
                                        bass.IndirectOffsetOnAxis(ap=item_ci[:, j:j + 1], axis=0)).then_inc(pairs_in, 16)
            pool.wait_ge(pairs_in, 16 * IC)
            stage_end(pool, 0)

            with pool.Fori(0, NI // 16) as g:
                for h in range(2):
                    turn(pool, idx_ready, 2 * g + h + 1)
                    for k in range(8 * h, 8 * h + 8):
                        pool.indirect_dma_start(rows[:, k * RS:k * RS + D], None, xn_d,
                                                bass.IndirectOffsetOnAxis(ap=src_stage[:, k:k + 1], axis=0)).then_inc(rows_in[k], 16)
            stage_end(pool, 1)
            stage_end(pool, 2)

            with pool.Fori(0, T // 2) as i:
                for k in range(2):
                    turn(pool, xt_in[k], 16 * i + 16)
                    turn(pool, x1_ready, 2 * i + k + 1)
                    pool.tensor_tensor(xs_s[k], x_s[k], cols(xn, 2 * i + k, D), ALU.add).then_inc(s1_ready, 1)
                    turn(pool, s1_ready, 2 * i + k + 1)
                    pool.tensor_tensor(xs_s[k], xs_s[k], be1_sb, ALU.add).then_inc(xs_ready, 1)
            stage_end(pool, 3)
            stage_end(pool, 4)
            stage_end(pool, 5)

            with pool.Fori(0, T // 5) as i:
                turn(pool, pos_ready, i + 1)
                for k in range(5):
                    turn(pool, sc_in[k], 16 * i + 16)
                    for c in range(2):
                        pool.indirect_dma_start(xs_d, bass.IndirectOffsetOnAxis(ap=pos_stage[:, 2 * k + c:2 * k + c + 1], axis=0),
                                                sc_rows[k], None).then_inc(sc_out[k], 16)
            for k in range(5):
                pool.wait_ge(sc_out[k], 32 * (T // 5))
            stage_end(pool, 6)
            stage_end(pool, 7)

            with pool.Fori(0, T // 5) as i:
                turn(pool, dpos_ready, i + 1)
                for k in range(5):
                    for c, slot in enumerate((d_y1[k], d_y2[k])):
                        pool.indirect_dma_start(slot, None, ys_d,
                                                bass.IndirectOffsetOnAxis(ap=pos_stage[:, 2 * k + c:2 * k + c + 1], axis=0)).then_inc(dy_in[k], 16)
            stage_end(pool, 8)

        @block.scalar
        def _(act):
            def std_of(k):
                act.wait_ge(var_ready[k], 1)
                act.activation(st["std"][:, :], st["var"][:, :], ACT.Sqrt).then_inc(std_ready[k], 1)

            act.wait_ge(nt_ready, 1)
            act.wait_ge(pairs_in, 16 * IC)
            act.activation(pairs_f.rearrange("p (j c) -> p j c", c=2 * P)[:, :, 0:P],
                           pairs_i.rearrange("p (j c) -> p j c", c=2 * P)[:, :, 0:P], ACT.Copy).then_inc(pairs_ready, 1)
            for j in range(IC):
                act.activation(pairs_f[:, j * 2 * P + P:(j + 1) * 2 * P], pairs_i[:, j * 2 * P + P:(j + 1) * 2 * P],
                               ACT.Identity, bias=item_nt[:, j:j + 1]).then_inc(pairs_ready, 1)
            act.wait_ge(tables_t, 2 * IC + 1)
            act.activation(item_ti[0:IC, :], bank[3][0:IC, P:2 * P], ACT.Copy).then_inc(ti_ready, 1)
            for b in range(0, IC, 4):
                n = min(4, IC - b) * P
                act.activation(item_src[:, b * P:b * P + n], bank[b // 4][:, 0:n], ACT.Copy)
                act.activation(item_dst[:, b * P:b * P + n], bank[4 + b // 4][:, 0:n], ACT.Copy)
            std_of(0)
            act.wait_ge(norm_ready[0], 1)
            with act.Fori(0, T // 2) as i:
                act.activation(cols(xn, 2 * i + 1, D), cols(xn, 2 * i + 1, D), ACT.Identity,
                               scale=cols(st["rstd"], 2 * i + 1, 1), bias=cols(st["nmr"], 2 * i + 1, 1)).then_inc(xn_odd, 1)
            stage_end(act, 0)

            with act.Fori(0, NI // 16) as g:
                for h in range(2):
                    turn(act, mm_done, 16 * g + 8 * h + 8)
                    act.activation(src_stage[:, 8 * h:8 * h + 8], item_src[:, bass.ds(16 * g + 8 * h, 8)], ACT.Copy).then_inc(idx_ready, 1)
            stage_end(act, 1)

            act.preload_act_table(ACT.Gelu)
            act.sem_inc(tt_ready, 2)
            act.sem_inc(gelu_done, 2)

            def step1(t):
                a = t + 1
                if a.inside(T):
                    turn(act, tr_done, a.n + 1)
                    act.activation(xn_s[a.slot], cols(xn, a.n, D), ACT.Copy).then_inc(xns_ready, 1)
                if t.inside(T):
                    turn(act, tr_done, t.n + 3)
                    turn(act, f_done, t.n + 1)
                    act.activation(aggx_t[t.slot], bank[t.slot][:, :], ACT.Copy).then_inc(tt_ready, 1)
                b = t + -1
                if b.inside(T):
                    turn(act, f_done, b.n + 3)
                    act.activation(acc_cols(b.n), bank[2 + b.slot][:, 0:D], ACT.Gelu).then_inc(gelu_done, 1)
            pipelined(act, T, 1, 1, step1)
            stage_end(act, 2)

            std_of(1)
            act.wait_ge(norm_ready[1], 1)
            with act.Fori(0, T // 2) as i:
                for k in range(2):
                    turn(act, ug_ready, 2 * i + k + 1)
                    act.activation(u_s[k], acc_cols(2 * i + k), ACT.Identity, scale=cols(st["rstd"], 2 * i + k, 1),
                                   bias=cols(st["nmr"], 2 * i + k, 1)).then_inc(u_ready, 1)
            stage_end(act, 3)

            std_of(2)
            act.wait_ge(norm_ready[2], 1)
            act.sem_inc(xn2_ready, 2)
            for k in range(2):
                act.sem_inc(xn2_out[k], 16)
            with act.Fori(0, T // 2) as i:
                for k in range(2):
                    turn(act, xn2_out[k], 16 * i + 16)
                    turn(act, tr2_done, 2 * i + k + 1)
                    act.activation(xn2_s[k], acc_cols(2 * i + k), ACT.Identity, scale=cols(st["rstd"], 2 * i + k, 1),
                                   bias=cols(st["nmr"], 2 * i + k, 1)).then_inc(xn2_ready, 1)
            stage_end(act, 4)

            act.wait_ge(diff_ready, 1)
            act.activation(ed[:, :], v2[:, :], ACT.Exp).then_inc(exp_ready, 1)
            stage_end(act, 5)

            with act.Fori(0, T // 5) as i:
                turn(act, pos_used, i + 1)
                act.activation(pos_stage[:, :], pos_i[:, bass.ds(10 * i, 10)], ACT.Copy).then_inc(pos_ready, 1)
                for k in range(5):
                    turn(act, sc_out[k], 32 * i + 32)
                act.sem_inc(pos_used, 1)
            stage_end(act, 6)

            act.sem_inc(ht_ready, 2)

            def step2(t):
                if t.inside(MT):
                    e = act.value_load(et_i[0:1, bass.ds(t.n, 1)] if not isinstance(t.n, int) else et_i[0:1, t.n:t.n + 1], min_val=0, max_val=E - 1)
                    turn(act, ht_done, t.n + 3)
                    turn(act, mm2_done, t.n + 1)
                    for f in range(KF):
                        ins = act.activation(h_t[t.slot][:, f * P:(f + 1) * P], bank[4 + t.slot][:, f * P:(f + 1) * P], ACT.Relu,
                                             bias=b1_sb[:, bass.ds(e * KF + f, 1)])
                    ins.then_inc(ht_ready, 1)
            pipelined(act, MT, 2, 1, step2)
            stage_end(act, 7)

            with act.Fori(0, T // 5) as i:
                act.activation(pos_stage[:, :], pos_i[:, bass.ds(10 * i, 10)], ACT.Copy).then_inc(dpos_ready, 1)
                turn(act, d_done, 5 * i + 5)
            std_of(3)
            act.wait_ge(norm_ready[3], 1)
            with act.Fori(0, T // 5) as i:
                for k in range(5):
                    act.activation(acc_cols(5 * i + k), acc_cols(5 * i + k), ACT.Identity, scale=cols(st["rstd"], 5 * i + k, 1),
                                   bias=cols(st["nmr"], 5 * i + k, 1)).then_inc(yn_ready, 1)
            stage_end(act, 8)

        @block.tensor
        def _(pe):
            pe.wait_ge(masks_ready, 2)
            pe.wait_ge(pairs_ready, 1 + IC)
            for j in range(IC):
                pe.transpose(bank[j // 4][:, j % 4 * P:(j % 4 + 1) * P], pairs_f[:, j * 2 * P:j * 2 * P + P], ident[:, :]).then_inc(tables_t, 1)
                pe.transpose(bank[4 + j // 4][:, j % 4 * P:(j % 4 + 1) * P], pairs_f[:, j * 2 * P + P:(j + 1) * 2 * P], ident[:, :]).then_inc(tables_t, 1)
            pe.wait_ge(tc_ready, 1)
            pe.transpose(bank[3][0:IC, P:2 * P], item_tc[:, :], ident[:, :]).then_inc(tables_t, 1)
            stage_end(pe, 0)

            pe.sem_inc(mm_done, 16)
            with pe.Fori(0, NI // 16) as g:
                for k in range(16):
                    if k % 8 == 0:
                        turn(pe, oh_ready, 16 * g + k + 8)
                    if k % 4 == 0:
                        turn(pe, acc_done, 16 * g + k + 4)
                    turn(pe, rows_in[k], 16 * g + 16)
                    pe.matmul(bank[k % 8][:, 0:DA], onehot[:, k * P:(k + 1) * P], rows[:, k * RS:k * RS + DA],
                              start=True, stop=True).then_inc(mm_done, 1)
            stage_end(pe, 1)

            pe.sem_inc(tr_done, 2)
            pe.sem_inc(f_done, 2)
            pe.wait_ge(late_in, 16 * 7)

            def step1(t):
                a = t + 1
                if a.inside(T):
                    turn(pe, agg_ready, a.n + 1)
                    turn(pe, xns_ready, a.n + 1)
                    turn(pe, tt_ready, a.n + 1)
                    for k in range(KD):
                        pe.transpose(bank[a.slot][:, k * P:(k + 1) * P], agg_s[a.slot][:, k * P:(k + 1) * P], ident[:, :])
                    for k in range(KD):
                        ins = pe.transpose(bank[a.slot][:, D + k * P:D + (k + 1) * P], xn_s[a.slot][:, k * P:(k + 1) * P], ident[:, :])
                    ins.then_inc(tr_done, 1)
                if t.inside(T):
                    turn(pe, tt_ready, t.n + 3)
                    turn(pe, gelu_done, t.n + 1)
                    f = bank[2 + t.slot][:, 0:D]
                    for k in range(KD):
                        pe.matmul(f, aggx_t[t.slot][:, k * P:(k + 1) * P], wl_sb[:, k * D:(k + 1) * D], start=k == 0, stop=False)
                    for k in range(KD):
                        pe.matmul(f, aggx_t[t.slot][:, D + k * P:D + (k + 1) * P], wr_sb[:, k * D:(k + 1) * D], start=False, stop=False)
                    pe.matmul(f, ones[0:1, :], bl_sb[0:1, :], start=False, stop=True).then_inc(f_done, 1)
            pipelined(pe, T, 1, 1, step1)
            stage_end(pe, 2)
            stage_end(pe, 3)

            pe.sem_inc(tr2_done, 2)

            def step3(t):
                a = t + 1
                if a.inside(T):
                    turn(pe, xn2_ready, a.n + 3)
                    turn(pe, t2_ready, a.n + 1)
                    for k in range(KD):
                        ins = pe.transpose(bank[a.slot][:, k * P:(k + 1) * P], xn2_s[a.slot][:, k * P:(k + 1) * P], ident[:, :])
                    ins.then_inc(tr2_done, 1)
                if t.inside(T):
                    turn(pe, t2_ready, t.n + 3)
                    turn(pe, lg_ready, t.n + 1)
                    g = bank[2 + t.slot][:, 0:E]
                    for k in range(KD):
                        pe.matmul(g, xn2_t[t.slot][:, k * P:(k + 1) * P], gw_sb[:, k * E:(k + 1) * E], start=k == 0, stop=False)
                    pe.matmul(g, ones[0:1, :], gb_sb[0:1, :], start=False, stop=True).then_inc(lg_done, 1)
            pipelined(pe, T, 1, 1, step3)
            stage_end(pe, 4)

            pe.wait_ge(both_ready, 1)
            half = TE // 2
            for m, mask in enumerate((below, ones)):
                for c in range(2):
                    pe.matmul(bank[2 * m + c][:, 0:half], mask[:, :], both[:, c * half:(c + 1) * half], start=True, stop=True).then_inc(counts_done, 1)
            stage_end(pe, 5)
            stage_end(pe, 6)

            pe.sem_inc(mm1_done, 2)
            pe.sem_inc(ht_done, 2)
            pe.sem_inc(mm2_done, 2)

            def expert(t):
                return pe.value_load(et_i[0:1, bass.ds(t.n, 1)] if not isinstance(t.n, int) else et_i[0:1, t.n:t.n + 1], min_val=0, max_val=E - 1)

            def step2(t):
                a, b, c = t + 2, t + 1, t + -1
                eb = expert(b) if b.inside(MT) else None
                ec = expert(c) if c.inside(MT) else None
                if a.inside(MT):
                    turn(pe, xi_in[a.slot], 16 * a.round + 16)
                    turn(pe, xit_ready, a.n + 1)
                    for k in range(KD):
                        ins = pe.transpose(bank[a.slot][:, k * P:(k + 1) * P], xi[a.slot][:, k * P:(k + 1) * P], ident[:, :])
                    ins.then_inc(xt_done, 1)
                if b.inside(MT):
                    turn(pe, xit_ready, b.n + 3)
                    turn(pe, h_ready, b.n + 1)
                    for k in range(KD):
                        ins = pe.matmul(bank[2 + b.slot][:, 0:F], xi_t[b.slot][:, k * P:(k + 1) * P],
                                        w1_sb[:, bass.ds(eb * (KD * F) + k * F, F)], start=k == 0, stop=k == KD - 1)
                    ins.then_inc(mm1_done, 1)
                if t.inside(MT):
                    turn(pe, h_ready, t.n + 3)
                    turn(pe, ht_ready, t.n + 1)
                    for k in range(KF):
                        ins = pe.transpose(bank[4 + t.slot][:, k * P:(k + 1) * P], h_sb[t.slot][:, k * P:(k + 1) * P], ident[:, :])
                    ins.then_inc(ht_done, 1)
                if c.inside(MT):
                    turn(pe, ht_ready, c.n + 3)
                    turn(pe, y_ready, c.n + 1)
                    for k in range(KF):
                        ins = pe.matmul(bank[6 + c.slot][:, 0:D], h_t[c.slot][:, k * P:(k + 1) * P],
                                        w2_sb[:, bass.ds(ec * (KF * D) + k * D, D)], start=k == 0, stop=k == KF - 1)
                    ins.then_inc(mm2_done, 1)
            pipelined(pe, MT, 2, 1, step2)
            stage_end(pe, 7)
            stage_end(pe, 8)

        @block.vector
        def _(dve):
            def then(_):
                dve.drain()

            def finish_stats(k):
                s = stats[:, :].rearrange("p (t s) -> p s t", s=6)
                dve.drain()
                dve.tensor_tensor(st["sum"][:, :], s[:, 1], s[:, 4], ALU.add)
                dve.tensor_tensor(st["dif"][:, :], s[:, 1], s[:, 4], ALU.subtract)
                then(dve.tensor_tensor(st["var"][:, :], s[:, 2], s[:, 5], ALU.add))
                then(dve.tensor_tensor(st["dif"][:, :], st["dif"][:, :], st["dif"][:, :], ALU.mult))
                then(dve.scalar_tensor_tensor(out=st["var"][:, :], in0=st["dif"][:, :], scalar=D / 4, in1=st["var"][:, :],
                                              op0=ALU.mult, op1=ALU.add))
                dve.tensor_scalar(st["var"][:, :], st["var"][:, :], 1.0 / D, EPS, ALU.mult, ALU.add).then_inc(var_ready[k], 1)
                dve.tensor_scalar(st["mean"][:, :], st["sum"][:, :], 0.5, None, ALU.mult)
                dve.wait_ge(std_ready[k], 1)
                then(dve.reciprocal(st["rstd"][:, :], st["std"][:, :]))
                dve.scalar_tensor_tensor(out=st["nmr"][:, :], in0=st["mean"][:, :], scalar=-1.0, in1=st["rstd"][:, :],
                                         op0=ALU.mult, op1=ALU.mult).then_inc(norm_ready[k], 1)
                dve.drain()

            dve.wait_ge(heads_in, 16)
            dve.wait_ge(consts_ready, 9)
            then(dve.tensor_scalar(head_i, head_i, 7, None, ALU.arith_shift_right))
            then(dve.tensor_tensor(starts, head_i, chunk_no, ALU.add))
            for j in range(IC):
                then(dve.tensor_scalar(junk[:, 0:CHUNKS - 1], starts[:, 1:CHUNKS], item_no[:, j:j + 1], None, ALU.is_le, ALU.add,
                                       accum_out=item_c[:, j:j + 1]))
            dve.tensor_copy(item_ci[:, :], item_c[:, :]).then_inc(chunk_ready, 1)
            then(dve.tensor_tensor(item_t[:, :], item_no[:, :], item_c[:, :], ALU.subtract))
            dve.tensor_scalar(item_nt[:, :], item_t[:, :], -float(P), None, ALU.mult).then_inc(nt_ready, 1)
            dve.tensor_scalar(item_tc[:, :], item_t[:, :], float(T - 1), None, ALU.min).then_inc(tc_ready, 1)
            for c in range(5):
                n = T // 5
                dve.wait_ge(x_in[c], 16)
                with dve.Fori(0, n) as i:
                    dve.bn_stats(stats[:, bass.ds((i + c * n) * 6, 6)], xn[:, bass.ds((i + c * n) * D, D)])
            finish_stats(0)
            with dve.Fori(0, T // 2) as i:
                dve.tensor_scalar(cols(xn, 2 * i, D), cols(xn, 2 * i, D), cols(st["mean"], 2 * i, 1), cols(st["rstd"], 2 * i, 1),
                                  ALU.subtract, ALU.mult).then_inc(xn_even, 1)
            dve.memset(item_dst[:, NI:NI + 8], -1.0)
            stage_end(dve, 0)

            dve.memset(rows.rearrange("p (k r) -> p k r", r=RS)[:, :, D:D + 1], 1.0)
            dve.wait_ge(acc_zero, 1)
            dve.sem_inc(acc_done, 8)
            dve.drain()

            def make_onehots(h, item0):
                for k in range(8):
                    dst = item_dst[:, bass.ds(item0 + k, 1)] if not isinstance(item0, int) else item_dst[:, item0 + k:item0 + k + 1]
                    s = 8 * h + k
                    dve.tensor_scalar(onehot[:, s * P:(s + 1) * P], iota[:, :], dst, None, ALU.is_equal).then_inc(oh_ready, 1)

            def accumulate(h, item0):
                _, tiles = nc.values_load_multi_w_load_instructions(
                    tile_of_item[0:1, bass.ds(item0, 8)], engines=(mybir.EngineType.DVE,), min_val=0, max_val=T - 1)
                for k in range(8):
                    if k % 4 == 0:
                        turn(dve, mm_done, item0 + k + 20)
                    a = acc[:, bass.ds(tiles[k] * DA, DA)]
                    dve.tensor_tensor(a, a, bank[k][:, 0:DA], ALU.add).then_inc(acc_done, 1)
                    dve.drain()

            make_onehots(0, 0)
            with dve.Fori(0, NI // 16) as g:
                for h in range(2):
                    turn(dve, mm_done, 16 * g + 8 * h + 16)
                    make_onehots(1 - h, 16 * g + 8 * h + 8)
                    accumulate(h, 16 * g + 8 * h)
            stage_end(dve, 1)

            deg = acc3[:, :, D:D + 1].rearrange("p t a -> p (t a)")
            then(dve.tensor_scalar(rdeg[:, :], deg, 1.0, None, ALU.max))
            then(dve.reciprocal(rdeg[:, :], rdeg[:, :]))

            def step1(t):
                a, b = t + 1, t + -1
                if a.inside(T):
                    turn(dve, tr_done, a.n + 1)
                    dve.tensor_scalar(agg_s[a.slot], acc_cols(a.n), cols(rdeg, a.n, 1), None, ALU.mult).then_inc(agg_ready, 1)
                if b.inside(T):
                    turn(dve, gelu_done, b.n + 3)
                    dve.bn_stats(cols(stats, b.n, 6), acc_cols(b.n))
            pipelined(dve, T, 1, 1, step1)
            stage_end(dve, 2)

            finish_stats(1)
            dve.sem_inc(ug_ready, 2)
            dve.sem_inc(x1_ready, 2)
            dve.wait_ge(late_in, 16 * 7)
            with dve.Fori(0, T // 2) as i:
                for k in range(2):
                    turn(dve, u_ready, 2 * i + k + 1)
                    dve.tensor_tensor(ug_s[k], u_s[k], g1_sb, ALU.mult).then_inc(ug_ready, 1)
                    dve.drain()
                    turn(dve, xs_ready, 2 * i + k + 1)
                    dve.tensor_tensor(acc_cols(2 * i + k), ug_s[k], xs_s[k], ALU.add).then_inc(x1_ready, 1)
                    dve.drain()
                    dve.bn_stats(cols(stats, 2 * i + k, 6), acc_cols(2 * i + k))
            stage_end(dve, 3)

            finish_stats(2)
            dve.sem_inc(t2_ready, 2)
            dve.sem_inc(lg_ready, 2)

            def step3(t):
                a = t + 1
                if a.inside(T):
                    turn(dve, tr2_done, a.n + 3)
                    if not isinstance(t.i, int) or a.n >= 2:
                        turn(dve, lg_done, a.n - 1)
                    dve.tensor_copy(xn2_t[a.slot], bank[a.slot][:, 0:D]).then_inc(t2_ready, 1)
                if t.inside(T):
                    turn(dve, lg_done, t.n + 1)
                    dve.tensor_copy(cols(logits, t.n, E), bank[2 + t.slot][:, 0:E]).then_inc(lg_ready, 1)
            pipelined(dve, T, 1, 1, step3)
            stage_end(dve, 4)

            def te(a):
                return a.rearrange("p (t e) -> p t e", e=E)

            def over_e(a):
                return a.rearrange("p (t a) -> p t a", a=1).to_broadcast([P, T, E])

            def over_t(a):
                return a.rearrange("p (a e) -> p a e", a=1).to_broadcast([P, T, E])

            for lg, v, i, oh in ((logits, v1, i1, oh1), (lg2, v2, i2, oh2)):
                then(dve.tensor_reduce(out=v[:, :], in_=te(lg), axis=AX.X, op=ALU.max))
                then(dve.tensor_tensor(te(eq), te(lg), over_e(v[:, :]), ALU.is_equal))
                then(dve.scalar_tensor_tensor(out=te(cand), in0=te(eq), scalar=-float(E), in1=over_t(e_no[:, :]), op0=ALU.mult, op1=ALU.add))
                then(dve.tensor_reduce(out=i[:, :], in_=te(cand), axis=AX.X, op=ALU.min))
                then(dve.tensor_tensor(te(oh), te(cand), over_e(i[:, :]), ALU.is_equal))
                if lg is logits:
                    then(dve.scalar_tensor_tensor(out=lg2, in0=oh, scalar=-3.0e38, in1=lg, op0=ALU.mult, op1=ALU.add))
            dve.tensor_tensor(both, oh1, oh2, ALU.add).then_inc(both_ready, 1)
            dve.tensor_tensor(v2[:, :], v2[:, :], v1[:, :], ALU.subtract).then_inc(diff_ready, 1)
            dve.wait_ge(exp_ready, 1)
            then(dve.tensor_scalar(p1[:, :], ed[:, :], 1.0, None, ALU.add))
            then(dve.reciprocal(p1[:, :], p1[:, :]))
            dve.tensor_tensor(p2[:, :], ed[:, :], p1[:, :], ALU.mult)
            dve.wait_ge(counts_done, 4)
            half = TE // 2
            for m, dst in enumerate((cum, tot)):
                for c in range(2):
                    dve.tensor_copy(dst[:, c * half:(c + 1) * half], bank[2 * m + c][:, 0:half])
            dve.drain()
            for e in range(E):
                dve.tensor_tensor_scan(te(inc)[:, :, e], ones[:, 0:T], te(tot)[:, :, e], 0.0, ALU.mult, ALU.add)
            dve.drain()
            then(dve.tensor_scalar(nt_i[:, :], inc[:, (T - 1) * E:T * E], float(P - 1), None, ALU.add))
            then(dve.tensor_scalar(nt_i[:, :], nt_i[:, :], 7, None, ALU.arith_shift_right))
            then(dve.tensor_copy(nt_f[:, :], nt_i[:, :]))
            then(dve.tensor_tensor_scan(end_f[:, :], ones[:, 0:E], nt_f[:, :], 0.0, ALU.mult, ALU.add))
            then(dve.tensor_tensor(base_f[:, :], end_f[:, :], nt_f[:, :], ALU.subtract))
            then(dve.tensor_scalar(base_f[:, :], base_f[:, :], float(P), None, ALU.mult))
            then(dve.tensor_tensor(pos_all, inc, tot, ALU.subtract))
            then(dve.tensor_tensor(pos_all, pos_all, cum, ALU.add))
            then(dve.tensor_tensor(te(pos_all), te(pos_all), over_t(base_f[:, :]), ALU.add))
            for c, oh in enumerate((oh1, oh2)):
                then(dve.tensor_tensor(prod, oh, pos_all, ALU.mult))
                then(dve.tensor_reduce(out=posf[:, :].rearrange("p (t c) -> p t c", c=2)[:, :, c], in_=te(prod), axis=AX.X, op=ALU.add))
            dve.tensor_copy(pos_i[:, :], posf[:, :])
            c3 = cmp_[0:1, :].rearrange("p (m e) -> p m e", e=E)
            then(dve.tensor_tensor(c3, end_f[0:1, :].rearrange("p (a e) -> p a e", a=1).to_broadcast([1, MT, E]),
                                   m_no[0:1, :].rearrange("p (m a) -> p m a", a=1).to_broadcast([1, MT, E]), ALU.is_le))
            then(dve.tensor_reduce(out=et_f[0:1, :], in_=c3, axis=AX.X, op=ALU.add))
            dve.tensor_scalar(et_i[0:1, :], et_f[0:1, :], float(E - 1), None, ALU.min)
            stage_end(dve, 5)
            dve.sem_inc(pos_used, 1)
            stage_end(dve, 6)

            dve.sem_inc(xit_ready, 2)
            dve.sem_inc(h_ready, 2)
            dve.sem_inc(y_ready, 2)
            for k in range(2):
                dve.sem_inc(y_out[k], 16)

            def step2(t):
                a, b, c = t + 2, t + 1, t + -1
                if a.inside(MT):
                    turn(dve, xt_done, a.n + 1)
                    turn(dve, mm1_done, a.n + 1)
                    dve.tensor_copy(xi_t[a.slot], bank[a.slot][:, 0:D]).then_inc(xit_ready, 1)
                if b.inside(MT):
                    turn(dve, mm1_done, b.n + 3)
                    turn(dve, ht_done, b.n + 1)
                    dve.tensor_copy(h_sb[b.slot], bank[2 + b.slot][:, 0:F]).then_inc(h_ready, 1)
                if c.inside(MT):
                    e = dve.value_load(et_i[0:1, bass.ds(c.n, 1)] if not isinstance(c.n, int) else et_i[0:1, c.n:c.n + 1], min_val=0, max_val=E - 1)
                    turn(dve, mm2_done, c.n + 3)
                    turn(dve, y_out[c.slot], 16 * c.round + 16)
                    dve.tensor_tensor(y_sb[c.slot], bank[6 + c.slot][:, 0:D], b2_sb[:, bass.ds(e * D, D)], ALU.add).then_inc(y_ready, 1)
            pipelined(dve, MT, 2, 1, step2)
            stage_end(dve, 7)

            with dve.Fori(0, T // 5) as i:
                for k in range(5):
                    n = 5 * i + k
                    turn(dve, d_in[k], 16 * i + 16)
                    turn(dve, dy_in[k], 32 * i + 32)
                    dve.scalar_tensor_tensor(out=d_t[k], in0=d_y1[k], scalar=cols(p1, n, 1), in1=d_x[k], op0=ALU.mult, op1=ALU.add)
                    dve.drain()
                    dve.scalar_tensor_tensor(out=acc_cols(n), in0=d_y2[k], scalar=cols(p2, n, 1), in1=d_t[k], op0=ALU.mult, op1=ALU.add).then_inc(d_done, 1)
                    dve.drain()
                    dve.bn_stats(cols(stats, n, 6), acc_cols(n))
            finish_stats(3)
            for k in range(5):
                dve.sem_inc(o_out[k], 16)
            with dve.Fori(0, T // 5) as i:
                for k in range(5):
                    n = 5 * i + k
                    turn(dve, yn_ready, n + 1)
                    turn(dve, o_in[k], 16 * i + 16)
                    a = acc_cols(n)
                    dve.tensor_tensor(a, a, g2_sb[:, :], ALU.mult)
                    dve.drain()
                    dve.tensor_tensor(a, a, be2_sb[:, :], ALU.add)
                    dve.drain()
                    turn(dve, o_out[k], 16 * i + 16)
                    dve.tensor_tensor(d_o[k], a, o_t[k], ALU.add).then_inc(o_ready, 1)
            stage_end(dve, 8)


def kernel(**inputs):
    import numpy as np
    import concourse.bacc as bacc
    from concourse.bass_utils import run_bass_kernel_spmd

    a = {name: np.asarray(v) for name, v in inputs.items()}
    nodes, d = a["x"].shape
    n_edges = a["src"].shape[0]
    chunks = -(-n_edges // 128)
    tiles = -(-nodes // 1280) * 10
    experts, _, f = a["L0_ffn_w1"].shape
    x = np.zeros((tiles * 128, d), np.float32)
    x[:nodes] = a["x"]
    edges = np.empty((2, chunks * 128), np.int32)
    edges[0, n_edges:], edges[1, n_edges:] = 0, nodes
    edges[0, :n_edges], edges[1, :n_edges] = a["src"], a["dst"]
    edges = edges.reshape(2, chunks, 128).transpose(1, 0, 2)
    arrays = {
        "x": x,
        "edges": edges.reshape(chunks, 256),
        "heads": edges[:, 1, 0].reshape(1, chunks),
        "w_l": a["L0_gnn_W_l"].T, "w_r": a["L0_gnn_W_r"].T, "b_l": a["L0_gnn_b_l"].reshape(1, d),
        "gamma1": a["L0_gnn_ln_gamma"].reshape(1, d), "beta1": a["L0_gnn_ln_beta"].reshape(1, d),
        "gate_w": a["L0_ffn_gate_w"], "gate_b": a["L0_ffn_gate_b"].reshape(1, experts),
        "w1": a["L0_ffn_w1"], "b1": a["L0_ffn_b1"].reshape(experts, f // 128, 128).transpose(2, 0, 1).reshape(128, -1),
        "w2": a["L0_ffn_w2"], "b2": a["L0_ffn_b2"].reshape(1, experts * d),
        "gamma2": a["L0_ffn_gamma"].reshape(1, d), "beta2": a["L0_ffn_beta"].reshape(1, d),
    }
    nc = bacc.Bacc("TRN2", target_bir_lowering=False, num_devices=1)
    arrays = {f"in_{name}": np.ascontiguousarray(v) for name, v in arrays.items()}
    args = [nc.dram_tensor(name, v.shape, mybir.dt.from_np(v.dtype), kind="ExternalInput").ap() for name, v in arrays.items()]
    out = nc.dram_tensor("out", (nodes, d), F32, kind="ExternalOutput").ap()
    build(nc, *args, out)
    r = run_bass_kernel_spmd(nc, [arrays], core_ids=[0])
    return r.results[0]["out"]
```

```python
from contextlib import ExitStack

import concourse.bass as bass
from concourse import mybir

F32 = mybir.dt.float32
I32 = mybir.dt.int32
ALU = mybir.AluOpType
ACT = mybir.ActivationFunctionType
AX = mybir.AxisListType

P = 128
EPS = 1e-5


class Tile:

    def __init__(self, i, c, unroll):
        self.i, self.c, self.unroll = i, c, unroll
        self.slot = c % 2
        self.n = unroll * i + c if isinstance(i, int) else i * unroll + c

    def __add__(self, k):
        return Tile(self.i, self.c + k, self.unroll)

    def inside(self, total):
        return not isinstance(self.i, int) or 0 <= self.n < total

    def slot_of(self, slots):
        return self.c % slots

    def uses(self, slots):
        assert self.unroll % slots == 0
        return self.i * (self.unroll // slots) + self.c // slots + 1


def pipelined(eng, total, before, after, step, unroll=2):
    first = -(-after // unroll) * unroll
    rounds = (total - before - first) // unroll
    for n in range(-before, first):
        step(Tile(0, n, unroll))
    with eng.Fori(0, rounds) as i:
        for c in range(unroll):
            step(Tile(i, first + c, unroll))
    for n in range(first + unroll * rounds, total + after):
        step(Tile(0, n, unroll))


def build(nc, x, src_t, dst_t, edges, heads, w_l, w_r, b_l, gamma1, beta1, gate_w, gate_b, w1, b1, w2, b2,
          gamma2, beta2, out):
    NODES, D = out.shape
    T = x.shape[0] // P
    CHUNKS = edges.shape[0]
    E, _, F = w1.shape
    KD, KF = D // P, F // P
    CPT = src_t.shape[1] // T
    MARGIN = 6
    RING, OHS = 11, 15
    PER_TILE = CPT + 2 * MARGIN
    assert CPT % RING == 0 and PER_TILE % OHS == 0 and 2 * MARGIN < CPT and T * CPT >= CHUNKS
    parts = [[k for k in (-1, 0, 1) if k == 0 or (k == -1 and j < MARGIN) or (k == 1 and j >= CPT - MARGIN)]
             for j in range(CPT)]
    ends = [sum(len(p) for p in parts[:j + 1]) for j in range(CPT)]
    NI = -(-(CHUNKS + T - 1) // P) * P
    IC = NI // P
    B = 7
    NB = T // B
    assert T == B * NB and T % 2 == 1
    MT = -(-((2 * T * P + E * (P - 1)) // P) // 4) * 4
    DA = D + 1
    RS = D + 4

    xn_d = nc.dram_tensor("xn_d", [T * P, D], F32).ap()
    xn2_d = nc.dram_tensor("xn2_d", [T * P, D], F32).ap()
    x1_d = nc.dram_tensor("x1_d", [T * P, D], F32).ap()
    xs_d = nc.dram_tensor("xs_d", [MT * P, D], F32).ap()
    ys_d = nc.dram_tensor("ys_d", [MT * P, D], F32).ap()
    tt_d = nc.dram_tensor("tt_d", [IC, P], I32).ap()

    with ExitStack() as ctx:
        def sb(name, cols, dt=F32):
            return ctx.enter_context(nc.sbuf_tensor(name, [P, cols], dt))

        def sem(name):
            return ctx.enter_context(nc.semaphore(name))

        bank = [ctx.enter_context(nc.psum_tensor(f"bank{i}", [P, 512], F32)) for i in range(8)]

        W1N, W2N = E * KD * F, E * KF * D
        big = sb("big", W1N + W2N)
        w1_sb = big[:, 0:W1N]
        w2_sb = big[:, W1N:W1N + W2N]
        cursor = [0]

        def part(base, cols):
            at = base + cursor[0]
            cursor[0] += cols
            assert cursor[0] <= W1N
            return big[:, at:at + cols]

        xn = part(0, T * D)
        cursor[0] = 0
        rows = part(0, RING * RS)
        onehot = part(0, OHS * P)
        cursor[0] = 0
        src_all = part(W1N, T * CPT).bitcast(I32)
        rel_all = part(W1N, T * CPT)
        dst_i = part(W1N, T * CPT).bitcast(I32)
        first_node = part(W1N, T * CPT)
        inside_ = part(W1N, T * CPT)
        cursor[0] = 0
        acc = part(0, T * DA)
        tile_of_item = part(0, NI).bitcast(I32)
        cursor[0] = 0
        item_src = part(W1N, NI).bitcast(I32)
        item_dst = part(W1N, NI + 8)
        kept = cursor[0]
        pairs_i = part(W1N, IC * 2 * P).bitcast(I32)
        pairs_f = part(W1N, IC * 2 * P)
        starts = part(W1N, CHUNKS)
        head_i = pairs_f[:, 0:CHUNKS].bitcast(I32)
        chunk_no = pairs_f[:, CHUNKS:2 * CHUNKS]
        junk = pairs_f[:, 0:CHUNKS]
        cursor[0] = kept
        rows_g = part(W1N, 16 * RS)
        onehot_g = part(W1N, 16 * P)
        cursor[0] = 0
        TE = T * E
        eq, cand, oh1, oh2, lg2, both, cum, tot, inc, pos_all, prod = [part(0, TE) for _ in range(11)]
        cmp_ = part(0, MT * E)
        cursor[0] = 0
        d_x, d_y1, d_y2, d_x1 = [[part(0, B * D) for _ in range(2)] for _ in range(4)]

        wl_sb = sb("wl_sb", KD * D)
        wr_sb = sb("wr_sb", KD * D)
        bl_sb = sb("bl_sb", D)
        g1_sb = sb("g1_sb", D)
        be1_sb = sb("be1_sb", D)
        gw_sb = sb("gw_sb", KD * E)
        gb_sb = sb("gb_sb", E)
        logits = sb("logits", T * E)
        nx, nxn, agg_s, f_s, s_s, x1_s, xn2_s, xn2_t = [sb(f"node_{n}", D) for n in ("x", "xn", "agg", "f", "s", "x1", "xn2", "xn2_t")]
        x1b_s = sb("node_x1b", D)
        aggx_t = sb("node_aggx_t", 2 * D)
        deg_s, nstat, nmv, nvar, nstd, nrstd = sb("deg_s", 1), sb("nstat", 6), sb("nmv", 2), sb("nvar", 1), sb("nstd", 1), sb("nrstd", 1)
        src_now = sb("src_now", 2 * CPT, I32)
        rel_now = sb("rel_now", 2 * CPT)
        flag_f, flag_i = sb("flag_f", 1), sb("flag_i", 1, I32)
        iota3 = sb("iota3", 3 * P)
        b2_sb = sb("b2_sb", E * D)
        cwork = sb("cwork", 8 * D + 4 * F)
        sc_rows = [cwork[:, k * B * D:(k + 1) * B * D] for k in range(2)]
        xi = [cwork[:, k * D:(k + 1) * D] for k in range(4)]
        xi_t = [cwork[:, (4 + k) * D:(5 + k) * D] for k in range(2)]
        y_sb = [cwork[:, (6 + k) * D:(7 + k) * D] for k in range(2)]
        h_sb = [cwork[:, 8 * D + k * F:8 * D + (k + 1) * F] for k in range(2)]
        h_t = [cwork[:, 8 * D + (2 + k) * F:8 * D + (3 + k) * F] for k in range(2)]
        d_stat, d_mv, d_var, d_std, d_rstd = [[sb(f"d_{n}{k}", B * w) for k in range(2)] for n, w in
                                              (("stat", 6), ("mv", 2), ("var", 1), ("std", 1), ("rstd", 1))]

        ident = sb("ident", P)
        iota = sb("iota", P)
        below = sb("below", P)
        ones = sb("ones", P)
        zeros = sb("zeros", D)
        g2_sb = sb("g2_sb", D)
        be2_sb = sb("be2_sb", D)
        b1_sb = sb("b1_sb", E * KF)
        stats = sb("stats", T * 6)
        st = {n: sb(f"st_{n}", T) for n in ("sum", "dif", "var", "std", "mean", "rstd", "nmr")}
        item_no = sb("item_no", IC)
        item_c = sb("item_c", IC)
        item_ci = sb("item_ci", IC, I32)
        item_t = sb("item_t", IC)
        item_nt = sb("item_nt", IC)
        item_tc = sb("item_tc", IC)
        item_ti = sb("item_ti", P, I32)
        src_stage = sb("src_stage", 16, I32)
        e_no = sb("e_no", E)
        m_no = sb("m_no", MT)
        v1, v2, i1, i2, p1, p2, ed = [sb(n, T) for n in ("v1", "v2", "i1", "i2", "p1", "p2", "ed")]
        posf = sb("posf", 2 * T)
        pos_i = sb("pos_i", 2 * T, I32)
        pos_stage = sb("pos_stage", 4 * B, I32)
        nt_i = sb("nt_i", E, I32)
        nt_f = sb("nt_f", E)
        end_f = sb("end_f", E)
        base_f = sb("base_f", E)
        et_f = sb("et_f", MT)
        et_i = sb("et_i", MT, I32)

        turns = sem("turns")
        stage = [sem(f"stage{i}_done") for i in range(9)]
        heads_in, params_in, late_in = sem("heads_in"), sem("params_in"), sem("late_in")
        x_in = [sem(f"x_in{i}") for i in range(NB)]
        chunkno_ready, consts_ready, masks_ready, acc_zero = sem("chunkno_ready"), sem("consts_ready"), sem("masks_ready"), sem("acc_zero")
        chunk_ready, nt_ready = sem("chunk_ready"), sem("nt_ready")
        pairs_in, pairs_ready, tables_t = sem("pairs_in"), sem("pairs_ready"), sem("tables_t")
        tc_ready, ti_ready, ti_out, ti_in = sem("tc_ready"), sem("ti_ready"), sem("ti_out"), sem("ti_in")
        var_ready, std_ready, norm_ready = sem("var_ready"), sem("std_ready"), sem("norm_ready")
        xn_even, xn_odd, xn_out = sem("xn_even"), sem("xn_odd"), sem("xn_out")
        idx_ready, oh_ready, mm_done, acc_done = sem("idx_ready"), sem("oh_ready"), sem("mm_done"), sem("acc_done")
        rows_in = [sem(f"rows_in{k}") for k in range(16)]
        w1_in, w2_in, b2_in, xs0_out = sem("w1_in"), sem("w2_in"), sem("b2_in"), sem("xs0_out")
        lo_ready, tables_in, ok_ready, ok_summed, flag_ready = sem("lo_ready"), sem("tables_in"), sem("ok_ready"), sem("ok_summed"), sem("flag_ready")
        now_ready, ohe_ready, mme_done = sem("now_ready"), sem("ohe_ready"), sem("mme_done")
        rowse_in = [sem(f"rowse_in{k}") for k in range(RING)]
        node_in, s_ready, agg_ready, nt_done, ntt_ready = sem("node_in"), sem("s_ready"), sem("agg_ready"), sem("nt_done"), sem("ntt_ready")
        f_done, gelu_done, var1_ready, std1_ready, var2_ready, std2_ready = [sem(n) for n in (
            "f_done", "gelu_done", "var1_ready", "std1_ready", "var2_ready", "std2_ready")]
        xn2_ready, x1b_ready, node_out, xn2t_done, xn2t_ready, lg_done, lg_ready = [sem(n) for n in (
            "xn2_ready", "x1b_ready", "node_out", "xn2t_done", "xn2t_ready", "lg_done", "lg_ready")]
        diff_ready, exp_ready, both_ready, counts_done = sem("diff_ready"), sem("exp_ready"), sem("both_ready"), sem("counts_done")
        sc_in, sc_out = [[sem(f"{n}{k}") for k in range(2)] for n in ("sc_in", "sc_out")]
        pos_ready = sem("pos_ready")
        xi_in = [sem(f"xi_in{k}") for k in range(4)]
        y_out = [sem(f"y_out{k}") for k in range(2)]
        xt_done, xit_ready, mm1_done, h_ready = sem("xt_done"), sem("xit_ready"), sem("mm1_done"), sem("h_ready")
        ht_done, ht_ready, mm2_done, y_ready = sem("ht_done"), sem("ht_ready"), sem("mm2_done"), sem("y_ready")
        dpos_ready, dvar_ready, dstd_ready, dout_ready = sem("dpos_ready"), sem("dvar_ready"), sem("dstd_ready"), sem("dout_ready")
        d_in, dy_in, d_out = [[sem(f"{n}{k}") for k in range(2)] for n in ("d_in", "dy_in", "d_out")]

        EVEN = (B + 1) // 2

        block = ctx.enter_context(nc.Block())

        def is_even(eng):
            return eng.If(eng.value_load(flag_i[0:1, 0:1], min_val=0, max_val=P) >= P)

        def turn(eng, s, value):
            if isinstance(value, int):
                if value > 0:
                    eng.wait_ge(s, value)
            else:
                eng.wait_ge(s, value)
                eng.sem_inc(turns, 1)

        def stage_end(eng, k):
            eng.drain().then_inc(stage[k], 1)
            eng.wait_ge(stage[k], 5)

        def cols(t, n, width):
            return t[:, bass.ds(n * width, width)] if not isinstance(n, int) else t[:, n * width:(n + 1) * width]

        def rows3(t, n):
            r = t[bass.ds(n * (B * P), B * P), :] if not isinstance(n, int) else t[n * B * P:(n + 1) * B * P, :]
            return r.rearrange("(t p) d -> p t d", p=P)

        def by_tile(a):
            return a.rearrange("p (t d) -> p t d", d=D)

        def dram_rows(t, n, count=P):
            return t[bass.ds(n * P, count), :] if not isinstance(n, int) else t[n * P:n * P + count, :]

        def w1_view():
            return w1_sb.rearrange("p (e k f) -> p e k f", e=E, k=KD), w1.rearrange("e (k p) f -> p e k f", p=P)

        def w2_view():
            return w2_sb.rearrange("p (e k h) -> p e k h", e=E, k=KF), w2.rearrange("e (k p) h -> p e k h", p=P)

        @block.sync
        def _(sp):
            sp.dma_start(dst_i, dst_t).then_inc(heads_in, 16)
            for c in range(NB):
                sp.dma_start(by_tile(cols(xn, c, B * D)), rows3(x, c)).then_inc(x_in[c], 16)
            sp.dma_start(src_all, src_t).then_inc(tables_in, 16)
            for dst, src in ((g2_sb, gamma2), (be2_sb, beta2), (g1_sb, gamma1), (be1_sb, beta1)):
                sp.dma_start(dst[:, :], src.to_broadcast([P, D])).then_inc(params_in, 16)
            sp.dma_start(b1_sb[:, :], b1).then_inc(params_in, 16)
            sp.dma_start(bl_sb[0:1, :], b_l).then_inc(params_in, 16)
            sp.dma_start(gb_sb[0:1, :], gate_b).then_inc(params_in, 16)
            for dst, src in ((wl_sb, w_l), (wr_sb, w_r), (gw_sb, gate_w)):
                sp.dma_start(dst[:, :].rearrange("p (k n) -> p k n", k=KD), src.rearrange("(k p) n -> p k n", p=P)).then_inc(params_in, 16)
            for c in range(NB):
                sp.wait_ge(xn_even, EVEN * (c + 1))
                sp.wait_ge(xn_odd, (B - EVEN) * (c + 1))
                sp.dma_start(rows3(xn_d, c), by_tile(cols(xn, c, B * D))).then_inc(xn_out, 16)
            sp.wait_ge(xn_out, 16 * NB)
            sp.wait_ge(tables_in, 16)
            sp.wait_ge(params_in, 16 * 10)
            stage_end(sp, 0)

            sp.dma_start(xs_d.rearrange("(p m) d -> p m d", p=P),
                         zeros[:, :].rearrange("p (a d) -> p a d", a=1).to_broadcast([P, MT, D])).then_inc(xs0_out, 16)

            def node_load(n):
                turn(sp, nt_done, n)
                turn(sp, s_ready, n)
                sp.dma_start(nxn[:, :], dram_rows(xn_d, n)).then_inc(node_in, 16)
                sp.dma_start(nx[:, :], dram_rows(x, n)).then_inc(node_in, 16)

            def node_store(n):
                turn(sp, xn2_ready, n + 1)
                sp.dma_start(dram_rows(xn2_d, n), xn2_s[:, :]).then_inc(node_out, 16)
                turn(sp, x1b_ready, n + 1)
                sp.dma_start(dram_rows(x1_d, n), x1b_s[:, :]).then_inc(node_out, 16)

            def node_both():
                with sp.Fori(0, T) as n:
                    node_load(n)
                    node_store(n)

            with is_even(sp):
                sp.dma_start(nxn[:, :], dram_rows(xn_d, 0)).then_inc(node_in, 16)
                sp.dma_start(nx[:, :], dram_rows(x, 0)).then_inc(node_in, 16)
                node_store(0)
                with sp.Fori(1, T) as n:
                    node_load(n)
                    node_store(n)
            with sp.Else():
                sp.dma_start(head_i, heads.to_broadcast([P, CHUNKS])).then_inc(heads_in, 16)
                sp.wait_ge(ti_ready, 1)
                sp.dma_start(tt_d, item_ti[0:IC, :]).then_inc(ti_out, 16)
                sp.wait_ge(ti_out, 16)
                sp.dma_start(tile_of_item[0:1, :], tt_d.rearrange("(a j) p -> a (j p)", a=1)).then_inc(ti_in, 16)
                sp.wait_ge(ti_in, 16)
                stage_end(sp, 1)
                stage_end(sp, 2)
                sp.dma_start(nxn[:, :], dram_rows(xn_d, 0)).then_inc(node_in, 16)
                sp.dma_start(nx[:, :], dram_rows(x, 0)).then_inc(node_in, 16)
                node_store(0)
                with sp.Fori(1, T) as n:
                    node_load(n)
                    node_store(n)
            sp.wait_ge(node_out, 32 * T)
            sp.wait_ge(xs0_out, 16)
            stage_end(sp, 4)
            stage_end(sp, 5)

            sp.dma_start(b2_sb[:, :], b2.to_broadcast([P, E * D])).then_inc(b2_in, 16)
            for n in range(2):
                sp.dma_start(by_tile(sc_rows[n][:, :]), rows3(xn2_d, n)).then_inc(sc_in[n], 16)
            w1_dst, w1_src = w1_view()
            w2_dst, w2_src = w2_view()
            for e in range(E):
                sp.dma_start(w1_dst[:, e], w1_src[:, e]).then_inc(w1_in, 16)
                sp.dma_start(w2_dst[:, e], w2_src[:, e]).then_inc(w2_in, 16)
            for n in range(2, NB):
                sp.wait_ge(sc_out[n % 2], 32 * B * (n // 2))
                sp.dma_start(by_tile(sc_rows[n % 2][:, :]), rows3(xn2_d, n)).then_inc(sc_in[n % 2], 16)
            sp.wait_ge(b2_in, 16)
            sp.wait_ge(w1_in, 16 * E)
            sp.wait_ge(w2_in, 16 * E)
            stage_end(sp, 6)

            def step2(t):
                a, c = t + 4, t + -3
                if a.inside(MT):
                    if not isinstance(t.n, int) or t.n >= 0:
                        turn(sp, xt_done, t.n + 1)
                    k = a.slot_of(4)
                    sp.dma_start(xi[k], dram_rows(xs_d, a.n)).then_inc(xi_in[k], 16)
                if c.inside(MT):
                    turn(sp, y_ready, c.n + 3)
                    sp.dma_start(dram_rows(ys_d, c.n), y_sb[c.slot]).then_inc(y_out[c.slot], 16)
            pipelined(sp, MT, 4, 3, step2, unroll=4)
            for k in range(2):
                sp.wait_ge(y_out[k], 16 * (MT // 2 + 1))
            stage_end(sp, 7)

            def d_load(n):
                k = n % 2
                if n >= 2:
                    sp.wait_ge(d_out[k], 16 * (n // 2))
                sp.dma_start(by_tile(d_x[k]), rows3(xn2_d, n)).then_inc(d_in[k], 16)
                sp.dma_start(by_tile(d_x1[k]), rows3(x1_d, n)).then_inc(d_in[k], 16)

            d_load(0)
            d_load(1)
            for n in range(NB):
                k = n % 2
                sp.wait_ge(dout_ready, n + 1)
                whole = min(NODES - n * B * P, B * P) // P
                res = by_tile(d_y1[k])
                sp.dma_start(out[n * B * P:(n * B + whole) * P, :].rearrange("(t p) d -> p t d", p=P), res[:, 0:whole]).then_inc(d_out[k], 16)
                if whole < B:
                    left = NODES - (n * B + whole) * P
                    sp.dma_start(out[(n * B + whole) * P:NODES, :], res[0:left, whole]).then_inc(d_out[k], 16)
                if n + 2 < NB:
                    d_load(n + 2)
            for k in range(2):
                sp.wait_ge(d_out[k], 16 * ((NB + 1 - k) // 2 + ((NB - 1) % 2 == k and NODES % P > 0)))
            stage_end(sp, 8)

        @block.gpsimd
        def _(pool):
            def count_up(t, pattern, base=0, channel_multiplier=0):
                return pool.iota(t, pattern=pattern, base=base, channel_multiplier=channel_multiplier, allow_small_or_imprecise_dtypes=True)

            count_up(first_node, [[P, T], [0, CPT]]).then_inc(consts_ready, 1)
            count_up(item_no[:, :], [[P, IC]], channel_multiplier=1).then_inc(consts_ready, 1)
            count_up(iota3[:, :], [[1, 3 * P]], base=-P).then_inc(consts_ready, 1)
            count_up(e_no[:, :], [[1, E]]).then_inc(consts_ready, 1)
            count_up(m_no[:, :], [[1, MT]]).then_inc(consts_ready, 1)
            pool.memset(ident[:, :], 0.0).then_inc(consts_ready, 1)
            pool.memset(below[:, :], 1.0).then_inc(consts_ready, 1)
            pool.memset(ones[:, :], 1.0).then_inc(consts_ready, 1)
            pool.memset(zeros[:, :], 0.0).then_inc(consts_ready, 1)
            pool.wait_ge(consts_ready, 9)
            pool.affine_select(out=ident[:, :], in_=ident[:, :], compare_op=ALU.not_equal, fill=1.0, base=0,
                               pattern=[[-1, P]], channel_multiplier=1).then_inc(masks_ready, 1)
            pool.affine_select(out=below[:, :], in_=below[:, :], compare_op=ALU.is_gt, fill=0.0, base=0,
                               pattern=[[1, P]], channel_multiplier=-1).then_inc(masks_ready, 1)
            stage_end(pool, 0)

            def gather_tile(t):
                turn(pool, now_ready, 2 * t.n + 2)
                for j in range(CPT):
                    turn(pool, mme_done, t.n * PER_TILE + (ends[j - RING] if j >= RING else ends[j - RING + CPT] - PER_TILE))
                    k = j % RING
                    at = t.slot * CPT + j
                    pool.indirect_dma_start(rows[:, k * RS:k * RS + D], None, xn_d,
                                            bass.IndirectOffsetOnAxis(ap=src_now[:, at:at + 1], axis=0)).then_inc(rowse_in[k], 16)

            with is_even(pool):
                gather_tile(Tile(0, 0, 2))
                with pool.Fori(0, (T - 1) // 2) as i:
                    gather_tile(Tile(i, 1, 2))
                    gather_tile(Tile(i, 2, 2))
            with pool.Else():
                count_up(chunk_no, [[1, CHUNKS]]).then_inc(chunkno_ready, 1)
                pool.memset(acc[:, :], 0.0).then_inc(acc_zero, 1)
                pool.wait_ge(chunk_ready, 1)
                for j in range(IC):
                    pool.indirect_dma_start(pairs_i[:, j * 2 * P:(j + 1) * 2 * P], None, edges,
                                            bass.IndirectOffsetOnAxis(ap=item_ci[:, j:j + 1], axis=0)).then_inc(pairs_in, 16)
                pool.wait_ge(pairs_in, 16 * IC)
                stage_end(pool, 1)
                with pool.Fori(0, NI // 16) as g:
                    for q in range(4):
                        turn(pool, idx_ready, 4 * g + q + 1)
                        for k in range(4 * q, 4 * q + 4):
                            pool.indirect_dma_start(rows_g[:, k * RS:k * RS + D], None, xn_d,
                                                    bass.IndirectOffsetOnAxis(ap=src_stage[:, k:k + 1], axis=0)).then_inc(rows_in[k], 16)
                stage_end(pool, 2)
            stage_end(pool, 4)
            stage_end(pool, 5)

            pool.wait_ge(pos_ready, 1)
            for n in range(NB):
                pool.wait_ge(sc_in[n % 2], 16 * (n // 2 + 1))
                for k in range(B):
                    for c in range(2):
                        at = (n * B + k) * 2 + c
                        pool.indirect_dma_start(xs_d, bass.IndirectOffsetOnAxis(ap=pos_i[:, at:at + 1], axis=0),
                                                sc_rows[n % 2][:, k * D:(k + 1) * D], None).then_inc(sc_out[n % 2], 16)
            for k in range(2):
                pool.wait_ge(sc_out[k], 32 * B * ((NB + 1 - k) // 2))
            stage_end(pool, 6)

            stage_end(pool, 7)

            for n in range(NB):
                if n >= 2:
                    pool.wait_ge(d_out[n % 2], 16 * (n // 2))
                for k in range(B):
                    for c, slot in enumerate((d_y1, d_y2)):
                        at = (n * B + k) * 2 + c
                        pool.indirect_dma_start(slot[n % 2][:, k * D:(k + 1) * D], None, ys_d,
                                                bass.IndirectOffsetOnAxis(ap=pos_i[:, at:at + 1], axis=0)).then_inc(dy_in[n % 2], 16)
            stage_end(pool, 8)

        @block.scalar
        def _(act):
            act.wait_ge(var_ready, 1)
            act.activation(st["std"][:, :], st["var"][:, :], ACT.Sqrt).then_inc(std_ready, 1)
            act.wait_ge(norm_ready, 1)
            with act.Fori(0, NB) as i:
                for k in range(EVEN, B):
                    n = B * i + k
                    act.activation(cols(xn, n, D), cols(xn, n, D), ACT.Identity,
                                   scale=cols(st["rstd"], n, 1), bias=cols(st["nmr"], n, 1)).then_inc(xn_odd, 1)
            stage_end(act, 0)

            def node_act(piece, n):
                if piece == "t":
                    turn(act, nt_done, n + 1)
                    act.activation(aggx_t[:, :], bank[2][:, :], ACT.Copy).then_inc(ntt_ready, 1)
                elif piece == "gelu":
                    turn(act, f_done, n + 1)
                    act.activation(f_s[:, :], bank[3][:, 0:D], ACT.Gelu).then_inc(gelu_done, 1)
                elif piece == "std1":
                    turn(act, var1_ready, n + 1)
                    act.activation(nstd[:, :], nvar[:, :], ACT.Sqrt).then_inc(std1_ready, 1)
                elif piece == "std2":
                    turn(act, var2_ready, n + 1)
                    act.activation(nstd[:, :], nvar[:, :], ACT.Sqrt).then_inc(std2_ready, 1)

            def stage_tile(t):
                turn(act, mme_done, (t.n - 1) * PER_TILE)
                act.activation(src_now[:, t.slot * CPT:(t.slot + 1) * CPT], cols(src_all, t.n, CPT), ACT.Copy).then_inc(now_ready, 1)
                act.activation(rel_now[:, t.slot * CPT:(t.slot + 1) * CPT], cols(rel_all, t.n, CPT), ACT.Copy).then_inc(now_ready, 1)

            with is_even(act):
                stage_tile(Tile(0, 0, 2))
                stage_tile(Tile(0, 1, 2))
                with act.Fori(0, (T - 3) // 2) as i:
                    for c in (2, 3):
                        t = Tile(i, c, 2)
                        stage_tile(t)
                        for piece in ("t", "gelu", "std1", "std2"):
                            node_act(piece, t.n - 2)
                stage_tile(Tile(0, T - 1, 2))
                for n in range(T - 3, T):
                    for piece in ("t", "gelu", "std1", "std2"):
                        node_act(piece, n)
            with act.Else():
                act.wait_ge(nt_ready, 1)
                act.wait_ge(pairs_in, 16 * IC)
                act.activation(pairs_f.rearrange("p (j c) -> p j c", c=2 * P)[:, :, 0:P],
                               pairs_i.rearrange("p (j c) -> p j c", c=2 * P)[:, :, 0:P], ACT.Copy).then_inc(pairs_ready, 1)
                for j in range(IC):
                    act.activation(pairs_f[:, j * 2 * P + P:(j + 1) * 2 * P], pairs_i[:, j * 2 * P + P:(j + 1) * 2 * P],
                                   ACT.Identity, bias=item_nt[:, j:j + 1]).then_inc(pairs_ready, 1)
                act.wait_ge(tables_t, 2 * IC + 1)
                act.activation(item_ti[0:IC, :], bank[3][0:IC, 2 * P:3 * P], ACT.Copy).then_inc(ti_ready, 1)
                for b in range(0, IC, 4):
                    n = min(4, IC - b) * P
                    act.activation(item_src[:, b * P:b * P + n], bank[b // 4][:, 0:n], ACT.Copy)
                    act.activation(item_dst[:, b * P:b * P + n], bank[4 + b // 4][:, 0:n], ACT.Copy)
                stage_end(act, 1)
                with act.Fori(0, NI // 16) as g:
                    for q in range(4):
                        turn(act, mm_done, 16 * g + 4 * q + 4)
                        act.activation(src_stage[:, 4 * q:4 * q + 4], item_src[:, bass.ds(16 * g + 4 * q, 4)], ACT.Copy).then_inc(idx_ready, 1)
                stage_end(act, 2)
                with act.Fori(0, T) as n:
                    for piece in ("t", "gelu", "std1", "std2"):
                        node_act(piece, n)
            stage_end(act, 4)

            act.wait_ge(diff_ready, 1)
            act.activation(ed[:, :], v2[:, :], ACT.Exp).then_inc(exp_ready, 1)
            stage_end(act, 5)

            act.sem_inc(pos_ready, 1)
            stage_end(act, 6)

            act.sem_inc(ht_ready, 2)

            def step2(t):
                if t.inside(MT):
                    e = act.value_load(et_i[0:1, bass.ds(t.n, 1)] if not isinstance(t.n, int) else et_i[0:1, t.n:t.n + 1], min_val=0, max_val=E - 1)
                    turn(act, ht_done, t.n + 3)
                    turn(act, mm2_done, t.n + 1)
                    for f in range(KF):
                        ins = act.activation(h_t[t.slot][:, f * P:(f + 1) * P], bank[4 + t.slot][:, f * P:(f + 1) * P], ACT.Relu,
                                             bias=b1_sb[:, bass.ds(e * KF + f, 1)])
                    ins.then_inc(ht_ready, 1)
            pipelined(act, MT, 2, 1, step2, unroll=4)
            stage_end(act, 7)

            for n in range(NB):
                act.wait_ge(dvar_ready, n + 1)
                act.activation(d_std[n % 2][:, :], d_var[n % 2][:, :], ACT.Sqrt).then_inc(dstd_ready, 1)
            stage_end(act, 8)

        @block.tensor
        def _(pe):
            pe.wait_ge(masks_ready, 2)
            pe.wait_ge(ok_ready, 1)
            pe.matmul(bank[0][0:1, 0:1], ones[:, 0:1], flag_f[:, :], start=True, stop=True).then_inc(ok_summed, 1)
            stage_end(pe, 0)

            def node_pe(piece, n):
                if piece == "transpose":
                    turn(pe, agg_ready, n + 1)
                    turn(pe, node_in, 32 * n + 32)
                    for k in range(KD):
                        pe.transpose(bank[2][:, k * P:(k + 1) * P], agg_s[:, k * P:(k + 1) * P], ident[:, :])
                    for k in range(KD):
                        ins = pe.transpose(bank[2][:, D + k * P:D + (k + 1) * P], nxn[:, k * P:(k + 1) * P], ident[:, :])
                    ins.then_inc(nt_done, 1)
                elif piece == "linear":
                    turn(pe, ntt_ready, n + 1)
                    f = bank[3][:, 0:D]
                    for k in range(KD):
                        pe.matmul(f, aggx_t[:, k * P:(k + 1) * P], wl_sb[:, k * D:(k + 1) * D], start=k == 0, stop=False)
                    for k in range(KD):
                        pe.matmul(f, aggx_t[:, D + k * P:D + (k + 1) * P], wr_sb[:, k * D:(k + 1) * D], start=False, stop=False)
                    pe.matmul(f, ones[0:1, :], bl_sb[0:1, :], start=False, stop=True).then_inc(f_done, 1)
                elif piece == "transpose2":
                    turn(pe, xn2_ready, n + 1)
                    for k in range(KD):
                        ins = pe.transpose(bank[4][:, k * P:(k + 1) * P], xn2_s[:, k * P:(k + 1) * P], ident[:, :])
                    ins.then_inc(xn2t_done, 1)
                elif piece == "gate":
                    turn(pe, xn2t_ready, n + 1)
                    g = bank[3][:, D:D + E]
                    for k in range(KD):
                        pe.matmul(g, xn2_t[:, k * P:(k + 1) * P], gw_sb[:, k * E:(k + 1) * E], start=k == 0, stop=False)
                    pe.matmul(g, ones[0:1, :], gb_sb[0:1, :], start=False, stop=True).then_inc(lg_done, 1)

            PE_AT = {10: "transpose", 13: "linear", 24: "transpose2", 28: "gate"}

            def sum_tile(t, first=False):
                for j in range(CPT):
                    if not first and j in PE_AT:
                        node_pe(PE_AT[j], t.n - 1)
                    turn(pe, ohe_ready, t.n * PER_TILE + ends[j])
                    k = j % RING
                    turn(pe, rowse_in[k], (t.n * (CPT // RING) + j // RING + 1) * 16)
                    for m, side in enumerate(parts[j]):
                        at = (ends[j] - len(parts[j]) + m) % OHS
                        starts_here = (side == 1 and j == CPT - MARGIN) or (first and j == 0)
                        ends_here = side == -1 and j == MARGIN - 1
                        pe.matmul(bank[(t.slot + side) % 2][:, 0:DA], onehot[:, at * P:(at + 1) * P], rows[:, k * RS:k * RS + DA],
                                  start=starts_here, stop=ends_here).then_inc(mme_done, 1)

            with is_even(pe):
                sum_tile(Tile(0, 0, 2), first=True)
                with pe.Fori(0, (T - 1) // 2) as i:
                    sum_tile(Tile(i, 1, 2))
                    sum_tile(Tile(i, 2, 2))
                for b in range(2):
                    pe.matmul(bank[b][:, 0:DA], zeros[:, 0:P], iota3[:, 0:DA], start=False, stop=True).then_inc(mme_done, 1)
                for piece in PE_AT.values():
                    node_pe(piece, T - 1)
            with pe.Else():
                pe.wait_ge(pairs_ready, 1 + IC)
                for j in range(IC):
                    pe.transpose(bank[j // 4][:, j % 4 * P:(j % 4 + 1) * P], pairs_f[:, j * 2 * P:j * 2 * P + P], ident[:, :]).then_inc(tables_t, 1)
                    pe.transpose(bank[4 + j // 4][:, j % 4 * P:(j % 4 + 1) * P], pairs_f[:, j * 2 * P + P:(j + 1) * 2 * P], ident[:, :]).then_inc(tables_t, 1)
                pe.wait_ge(tc_ready, 1)
                assert 12 < IC <= 14
                pe.transpose(bank[3][0:IC, 2 * P:3 * P], item_tc[:, :], ident[:, :]).then_inc(tables_t, 1)
                stage_end(pe, 1)
                pe.sem_inc(mm_done, 16)
                with pe.Fori(0, NI // 16) as g:
                    for k in range(16):
                        if k % 4 == 0:
                            turn(pe, oh_ready, 16 * g + k + 4)
                            turn(pe, acc_done, 16 * g + k + 4)
                        turn(pe, rows_in[k], 16 * g + 16)
                        pe.matmul(bank[k % 8][:, 0:DA], onehot_g[:, k * P:(k + 1) * P], rows_g[:, k * RS:k * RS + DA],
                                  start=True, stop=True).then_inc(mm_done, 1)
                stage_end(pe, 2)
                with pe.Fori(0, T) as n:
                    for piece in PE_AT.values():
                        node_pe(piece, n)
            stage_end(pe, 4)

            pe.wait_ge(both_ready, 1)
            half = T // 2 * E
            halves = ((0, half), (half, TE))
            for m, mask in enumerate((below, ones)):
                for c, (a, b) in enumerate(halves):
                    pe.matmul(bank[2 * m + c][:, 0:b - a], mask[:, :], both[:, a:b], start=True, stop=True).then_inc(counts_done, 1)
            stage_end(pe, 5)
            stage_end(pe, 6)

            pe.sem_inc(mm1_done, 2)
            pe.sem_inc(ht_done, 2)
            pe.sem_inc(mm2_done, 2)

            def expert(t):
                return pe.value_load(et_i[0:1, bass.ds(t.n, 1)] if not isinstance(t.n, int) else et_i[0:1, t.n:t.n + 1], min_val=0, max_val=E - 1)

            def step2(t):
                a, b, c = t + 2, t + 1, t + -1
                eb = expert(b) if b.inside(MT) else None
                ec = expert(c) if c.inside(MT) else None
                if a.inside(MT):
                    turn(pe, xi_in[a.slot_of(4)], 16 * a.uses(4))
                    turn(pe, xit_ready, a.n + 1)
                    for k in range(KD):
                        ins = pe.transpose(bank[a.slot][:, k * P:(k + 1) * P], xi[a.slot_of(4)][:, k * P:(k + 1) * P], ident[:, :])
                    ins.then_inc(xt_done, 1)
                if b.inside(MT):
                    turn(pe, xit_ready, b.n + 3)
                    turn(pe, h_ready, b.n + 1)
                    for k in range(KD):
                        ins = pe.matmul(bank[2 + b.slot][:, 0:F], xi_t[b.slot][:, k * P:(k + 1) * P],
                                        w1_sb[:, bass.ds(eb * (KD * F) + k * F, F)], start=k == 0, stop=k == KD - 1)
                    ins.then_inc(mm1_done, 1)
                if t.inside(MT):
                    turn(pe, h_ready, t.n + 3)
                    turn(pe, ht_ready, t.n + 1)
                    for k in range(KF):
                        ins = pe.transpose(bank[4 + t.slot][:, k * P:(k + 1) * P], h_sb[t.slot][:, k * P:(k + 1) * P], ident[:, :])
                    ins.then_inc(ht_done, 1)
                if c.inside(MT):
                    turn(pe, ht_ready, c.n + 3)
                    turn(pe, y_ready, c.n + 1)
                    for k in range(KF):
                        ins = pe.matmul(bank[6 + c.slot][:, 0:D], h_t[c.slot][:, k * P:(k + 1) * P],
                                        w2_sb[:, bass.ds(ec * (KF * D) + k * D, D)], start=k == 0, stop=k == KF - 1)
                    ins.then_inc(mm2_done, 1)
            pipelined(pe, MT, 2, 1, step2, unroll=4)
            stage_end(pe, 7)
            stage_end(pe, 8)

        @block.vector
        def _(dve):
            def then(_):
                dve.drain()

            def var_of(stat, mv, var):
                then(dve.bn_aggr(mv, stat))
                return dve.tensor_scalar(var, mv[:, 1:2], EPS, None, ALU.add)

            dve.wait_ge(consts_ready, 9)
            dve.wait_ge(heads_in, 16)
            then(dve.tensor_tensor(rel_all, dst_i, first_node, ALU.subtract))
            r3, b3, i3 = [a.rearrange("p (t j) -> p t j", j=CPT) for a in (rel_all, first_node, inside_)]
            then(dve.memset(first_node, 0.0))
            then(dve.memset(b3[:, :, 0:MARGIN], -float(P)))
            then(dve.tensor_tensor(inside_, rel_all, first_node, ALU.is_ge))
            then(dve.memset(first_node, float(P)))
            then(dve.memset(b3[:, :, CPT - MARGIN:CPT], 2.0 * P))
            then(dve.tensor_tensor(first_node, rel_all, first_node, ALU.is_lt))
            then(dve.tensor_tensor(inside_, inside_, first_node, ALU.mult))
            dve.tensor_reduce(out=flag_f[:, :], in_=inside_, axis=AX.X, op=ALU.min).then_inc(ok_ready, 1)
            for c in range(NB):
                dve.wait_ge(x_in[c], 16)
                with dve.Fori(0, B) as i:
                    dve.bn_stats(stats[:, bass.ds((i + c * B) * 6, 6)], xn[:, bass.ds((i + c * B) * D, D)])
            s = stats[:, :].rearrange("p (t s) -> p s t", s=6)
            dve.drain()
            dve.tensor_tensor(st["sum"][:, :], s[:, 1], s[:, 4], ALU.add)
            dve.tensor_tensor(st["dif"][:, :], s[:, 1], s[:, 4], ALU.subtract)
            then(dve.tensor_tensor(st["var"][:, :], s[:, 2], s[:, 5], ALU.add))
            then(dve.tensor_tensor(st["dif"][:, :], st["dif"][:, :], st["dif"][:, :], ALU.mult))
            then(dve.scalar_tensor_tensor(out=st["var"][:, :], in0=st["dif"][:, :], scalar=D / 4, in1=st["var"][:, :],
                                          op0=ALU.mult, op1=ALU.add))
            dve.tensor_scalar(st["var"][:, :], st["var"][:, :], 1.0 / D, EPS, ALU.mult, ALU.add).then_inc(var_ready, 1)
            dve.tensor_scalar(st["mean"][:, :], st["sum"][:, :], 0.5, None, ALU.mult)
            dve.wait_ge(std_ready, 1)
            then(dve.reciprocal(st["rstd"][:, :], st["std"][:, :]))
            then(dve.scalar_tensor_tensor(out=st["nmr"][:, :], in0=st["mean"][:, :], scalar=-1.0, in1=st["rstd"][:, :],
                                          op0=ALU.mult, op1=ALU.mult).then_inc(norm_ready, 1))
            with dve.Fori(0, NB) as i:
                for k in range(EVEN):
                    n = B * i + k
                    dve.tensor_scalar(cols(xn, n, D), cols(xn, n, D), cols(st["mean"], n, 1), cols(st["rstd"], n, 1),
                                      ALU.subtract, ALU.mult).then_inc(xn_even, 1)
            dve.wait_ge(ok_summed, 1)
            then(dve.tensor_copy(flag_i[0:1, :], bank[0][0:1, 0:1]))
            stage_end(dve, 0)

            def node_dve(piece, n, total=None):
                if piece == "s":
                    turn(dve, node_in, 32 * n + 32)
                    then(dve.tensor_tensor(s_s[:, :], nx[:, :], nxn[:, :], ALU.add).then_inc(s_ready, 1))
                    dve.tensor_tensor(s_s[:, :], s_s[:, :], be1_sb[:, :], ALU.add)
                elif piece == "mean":
                    then(dve.tensor_scalar(deg_s[:, :], total[:, D:DA], 1.0, None, ALU.max))
                    then(dve.reciprocal(deg_s[:, :], deg_s[:, :]))
                    dve.tensor_scalar(agg_s[:, :], total[:, 0:D], deg_s[:, :], None, ALU.mult).then_inc(agg_ready, 1)
                elif piece == "stats1":
                    turn(dve, gelu_done, n + 1)
                    then(dve.bn_stats(nstat[:, :], f_s[:, :]))
                    then(var_of(nstat[:, :], nmv[:, :], nvar[:, :]).then_inc(var1_ready, 1))
                elif piece == "x1":
                    turn(dve, std1_ready, n + 1)
                    then(dve.reciprocal(nrstd[:, :], nstd[:, :]))
                    then(dve.tensor_scalar(f_s[:, :], f_s[:, :], nmv[:, 0:1], nrstd[:, :], ALU.subtract, ALU.mult))
                    then(dve.tensor_tensor(f_s[:, :], f_s[:, :], g1_sb[:, :], ALU.mult))
                    then(dve.tensor_tensor(x1_s[:, :], f_s[:, :], s_s[:, :], ALU.add))
                    then(dve.bn_stats(nstat[:, :], x1_s[:, :]))
                    then(var_of(nstat[:, :], nmv[:, :], nvar[:, :]).then_inc(var2_ready, 1))
                elif piece == "xn2":
                    turn(dve, std2_ready, n + 1)
                    turn(dve, node_out, 32 * n)
                    then(dve.reciprocal(nrstd[:, :], nstd[:, :]))
                    dve.tensor_scalar(xn2_s[:, :], x1_s[:, :], nmv[:, 0:1], nrstd[:, :], ALU.subtract, ALU.mult).then_inc(xn2_ready, 1)
                    dve.tensor_tensor(x1b_s[:, :], x1_s[:, :], be2_sb[:, :], ALU.add).then_inc(x1b_ready, 1)
                elif piece == "xn2t":
                    turn(dve, xn2t_done, n + 1)
                    dve.tensor_copy(xn2_t[:, :], bank[4][:, 0:D]).then_inc(xn2t_ready, 1)
                elif piece == "logits":
                    turn(dve, lg_done, n + 1)
                    dve.tensor_copy(cols(logits, n, E), bank[3][:, D:D + E]).then_inc(lg_ready, 1)

            DVE_AT = {5: "s", 8: "mean", 17: "stats1", 20: "x1", 23: "xn2", 26: "xn2t", 31: "logits"}
            order = list(DVE_AT.values())

            def onehots_of(t, first=False):
                turn(dve, now_ready, 2 * t.n + 2)
                for j in range(CPT):
                    if not first and j in DVE_AT:
                        if DVE_AT[j] == "mean":
                            turn(dve, mme_done, t.n * PER_TILE + ends[MARGIN - 1])
                        node_dve(DVE_AT[j], t.n - 1, bank[(t.slot + 1) % 2])
                    turn(dve, mme_done, t.n * PER_TILE + (ends[j] - OHS))
                    for m, side in enumerate(parts[j]):
                        at = (ends[j] - len(parts[j]) + m) % OHS
                        dve.tensor_scalar(onehot[:, at * P:(at + 1) * P], iota3[:, (side + 1) * P:(side + 2) * P],
                                          rel_now[:, t.slot * CPT + j:t.slot * CPT + j + 1], None, ALU.is_equal).then_inc(ohe_ready, 1)

            with is_even(dve):
                then(dve.memset(rows.rearrange("p (k r) -> p k r", r=RS)[:, :, D:D + 1], 1.0))
                onehots_of(Tile(0, 0, 2), first=True)
                with dve.Fori(0, (T - 1) // 2) as i:
                    onehots_of(Tile(i, 1, 2))
                    onehots_of(Tile(i, 2, 2))
                dve.wait_ge(mme_done, T * PER_TILE + 2)
                for piece in order:
                    node_dve(piece, T - 1, bank[(T - 1) % 2])
            with dve.Else():
                dve.wait_ge(heads_in, 32)
                dve.wait_ge(chunkno_ready, 1)
                then(dve.tensor_scalar(head_i, head_i, 7, None, ALU.arith_shift_right))
                then(dve.tensor_tensor(starts, head_i, chunk_no, ALU.add))
                for j in range(IC):
                    then(dve.tensor_scalar(junk[:, 0:CHUNKS - 1], starts[:, 1:CHUNKS], item_no[:, j:j + 1], None, ALU.is_le, ALU.add,
                                           accum_out=item_c[:, j:j + 1]))
                then(dve.tensor_copy(item_ci[:, :], item_c[:, :]).then_inc(chunk_ready, 1))
                then(dve.tensor_tensor(item_t[:, :], item_no[:, :], item_c[:, :], ALU.subtract))
                dve.tensor_scalar(item_nt[:, :], item_t[:, :], -float(P), None, ALU.mult).then_inc(nt_ready, 1)
                dve.tensor_scalar(item_tc[:, :], item_t[:, :], float(T - 1), None, ALU.min).then_inc(tc_ready, 1)
                dve.memset(item_dst[:, NI:NI + 8], -1.0)
                stage_end(dve, 1)

                dve.memset(rows_g.rearrange("p (k r) -> p k r", r=RS)[:, :, D:D + 1], 1.0)
                dve.wait_ge(acc_zero, 1)
                dve.sem_inc(acc_done, 8)
                dve.drain()

                def make_onehots(q, item0):
                    for k in range(4):
                        dst = item_dst[:, bass.ds(item0 + k, 1)] if not isinstance(item0, int) else item_dst[:, item0 + k:item0 + k + 1]
                        s = 4 * q + k
                        dve.tensor_scalar(onehot_g[:, s * P:(s + 1) * P], iota3[:, P:2 * P], dst, None, ALU.is_equal).then_inc(oh_ready, 1)

                def accumulate(q, item0):
                    _, tiles = nc.values_load_multi_w_load_instructions(
                        tile_of_item[0:1, bass.ds(item0, 4)], engines=(mybir.EngineType.DVE,), min_val=0, max_val=T - 1)
                    turn(dve, mm_done, item0 + 20)
                    for k in range(4):
                        a = acc[:, bass.ds(tiles[k] * DA, DA)]
                        dve.tensor_tensor(a, a, bank[4 * (q % 2) + k][:, 0:DA], ALU.add).then_inc(acc_done, 1)
                        dve.drain()

                for q in range(2):
                    make_onehots(q, 4 * q)
                with dve.Fori(0, NI // 16) as g:
                    for q in range(4):
                        make_onehots((q + 2) % 4, 16 * g + 4 * q + 8)
                        accumulate(q, 16 * g + 4 * q)
                stage_end(dve, 2)
                with dve.Fori(0, T) as n:
                    for piece in order:
                        node_dve(piece, n, acc[:, bass.ds(n * DA, DA)])
            stage_end(dve, 4)

            def te(a):
                return a.rearrange("p (t e) -> p t e", e=E)

            def over_e(a):
                return a.rearrange("p (t a) -> p t a", a=1).to_broadcast([P, T, E])

            def over_t(a):
                return a.rearrange("p (a e) -> p a e", a=1).to_broadcast([P, T, E])

            for lg, v, i, oh in ((logits[:, :], v1, i1, oh1), (lg2, v2, i2, oh2)):
                then(dve.tensor_reduce(out=v[:, :], in_=te(lg), axis=AX.X, op=ALU.max))
                then(dve.tensor_tensor(te(eq), te(lg), over_e(v[:, :]), ALU.is_equal))
                then(dve.scalar_tensor_tensor(out=te(cand), in0=te(eq), scalar=-float(E), in1=over_t(e_no[:, :]), op0=ALU.mult, op1=ALU.add))
                then(dve.tensor_reduce(out=i[:, :], in_=te(cand), axis=AX.X, op=ALU.min))
                then(dve.tensor_tensor(te(oh), te(cand), over_e(i[:, :]), ALU.is_equal))
                if oh is oh1:
                    then(dve.scalar_tensor_tensor(out=lg2, in0=oh, scalar=-3.0e38, in1=lg, op0=ALU.mult, op1=ALU.add))
            dve.tensor_tensor(both, oh1, oh2, ALU.add).then_inc(both_ready, 1)
            dve.tensor_tensor(v2[:, :], v2[:, :], v1[:, :], ALU.subtract).then_inc(diff_ready, 1)
            dve.wait_ge(exp_ready, 1)
            then(dve.tensor_scalar(p1[:, :], ed[:, :], 1.0, None, ALU.add))
            then(dve.reciprocal(p1[:, :], p1[:, :]))
            dve.tensor_tensor(p2[:, :], ed[:, :], p1[:, :], ALU.mult)
            dve.wait_ge(counts_done, 4)
            half = T // 2 * E
            halves = ((0, half), (half, TE))
            for m, dst in enumerate((cum, tot)):
                for c, (a, b) in enumerate(halves):
                    dve.tensor_copy(dst[:, a:b], bank[2 * m + c][:, 0:b - a])
            dve.drain()
            for e in range(E):
                dve.tensor_tensor_scan(te(inc)[:, :, e], ones[:, 0:T], te(tot)[:, :, e], 0.0, ALU.mult, ALU.add)
            dve.drain()
            then(dve.tensor_scalar(nt_i[:, :], inc[:, (T - 1) * E:T * E], float(P - 1), None, ALU.add))
            then(dve.tensor_scalar(nt_i[:, :], nt_i[:, :], 7, None, ALU.arith_shift_right))
            then(dve.tensor_copy(nt_f[:, :], nt_i[:, :]))
            then(dve.tensor_tensor_scan(end_f[:, :], ones[:, 0:E], nt_f[:, :], 0.0, ALU.mult, ALU.add))
            then(dve.tensor_tensor(base_f[:, :], end_f[:, :], nt_f[:, :], ALU.subtract))
            then(dve.tensor_scalar(base_f[:, :], base_f[:, :], float(P), None, ALU.mult))
            then(dve.tensor_tensor(pos_all, inc, tot, ALU.subtract))
            then(dve.tensor_tensor(pos_all, pos_all, cum, ALU.add))
            then(dve.tensor_tensor(te(pos_all), te(pos_all), over_t(base_f[:, :]), ALU.add))
            for c, oh in enumerate((oh1, oh2)):
                then(dve.tensor_tensor(prod, oh, pos_all, ALU.mult))
                then(dve.tensor_reduce(out=posf[:, :].rearrange("p (t c) -> p t c", c=2)[:, :, c], in_=te(prod), axis=AX.X, op=ALU.add))
            dve.tensor_copy(pos_i[:, :], posf[:, :])
            c3 = cmp_[0:1, :].rearrange("p (m e) -> p m e", e=E)
            then(dve.tensor_tensor(c3, end_f[0:1, :].rearrange("p (a e) -> p a e", a=1).to_broadcast([1, MT, E]),
                                   m_no[0:1, :].rearrange("p (m a) -> p m a", a=1).to_broadcast([1, MT, E]), ALU.is_le))
            then(dve.tensor_reduce(out=et_f[0:1, :], in_=c3, axis=AX.X, op=ALU.add))
            dve.tensor_scalar(et_i[0:1, :], et_f[0:1, :], float(E - 1), None, ALU.min)
            stage_end(dve, 5)
            stage_end(dve, 6)

            dve.sem_inc(xit_ready, 2)
            dve.sem_inc(h_ready, 2)
            dve.sem_inc(y_ready, 2)
            for k in range(2):
                dve.sem_inc(y_out[k], 16)

            def step2(t):
                a, b, c = t + 2, t + 1, t + -1
                if a.inside(MT):
                    turn(dve, xt_done, a.n + 1)
                    turn(dve, mm1_done, a.n + 1)
                    dve.tensor_copy(xi_t[a.slot], bank[a.slot][:, 0:D]).then_inc(xit_ready, 1)
                if b.inside(MT):
                    turn(dve, mm1_done, b.n + 3)
                    turn(dve, ht_done, b.n + 1)
                    dve.tensor_copy(h_sb[b.slot], bank[2 + b.slot][:, 0:F]).then_inc(h_ready, 1)
                if c.inside(MT):
                    e = dve.value_load(et_i[0:1, bass.ds(c.n, 1)] if not isinstance(c.n, int) else et_i[0:1, c.n:c.n + 1], min_val=0, max_val=E - 1)
                    turn(dve, mm2_done, c.n + 3)
                    turn(dve, y_out[c.slot], 16 * c.uses(2))
                    dve.tensor_tensor(y_sb[c.slot], bank[6 + c.slot][:, 0:D], b2_sb[:, bass.ds(e * D, D)], ALU.add).then_inc(y_ready, 1)
            pipelined(dve, MT, 2, 1, step2, unroll=4)
            stage_end(dve, 7)

            def combine(n):
                k = n % 2
                y1, y2, xx = by_tile(d_y1[k]), by_tile(d_y2[k]), by_tile(d_x[k])
                dve.wait_ge(d_in[k], 32 * (n // 2 + 1))
                dve.wait_ge(dy_in[k], 32 * B * (n // 2 + 1))
                for c, yc in enumerate((y1, y2)):
                    for b in range(B):
                        w = (p1, p2)[c][:, n * B + b:n * B + b + 1]
                        dve.scalar_tensor_tensor(out=xx[:, b], in0=yc[:, b], scalar=w, in1=xx[:, b], op0=ALU.mult, op1=ALU.add)
                    dve.drain()
                for b in range(B):
                    dve.bn_stats(d_stat[k][:, 6 * b:6 * b + 6], xx[:, b])
                dve.drain()
                for b in range(B):
                    dve.bn_aggr(d_mv[k][:, 2 * b:2 * b + 2], d_stat[k][:, 6 * b:6 * b + 6])
                dve.drain()
                dve.tensor_scalar(d_var[k][:, :], d_mv[k][:, :].rearrange("p (b c) -> p b c", c=2)[:, :, 1], EPS, None, ALU.add).then_inc(dvar_ready, 1)

            def normalise(n):
                k = n % 2
                y1, xx = by_tile(d_y1[k]), by_tile(d_x[k])
                dve.wait_ge(dstd_ready, n + 1)
                then(dve.reciprocal(d_rstd[k][:, :], d_std[k][:, :]))
                for b in range(B):
                    dve.tensor_scalar(xx[:, b], xx[:, b], d_mv[k][:, 2 * b:2 * b + 1], d_rstd[k][:, b:b + 1], ALU.subtract, ALU.mult)
                dve.drain()
                g = g2_sb[:, :].rearrange("p (a d) -> p a d", a=1).to_broadcast([P, B, D])
                then(dve.tensor_tensor(y1, xx, g, ALU.mult))
                dve.tensor_tensor(y1, y1, by_tile(d_x1[k]), ALU.add).then_inc(dout_ready, 1)

            for n in range(NB + 1):
                if n < NB:
                    combine(n)
                if n > 0:
                    normalise(n - 1)
            stage_end(dve, 8)


def kernel(**inputs):
    import numpy as np
    import concourse.bacc as bacc
    from concourse.bass_utils import run_bass_kernel_spmd

    a = {name: np.asarray(v) for name, v in inputs.items()}
    nodes, d = a["x"].shape
    n_edges = a["src"].shape[0]
    chunks = -(-n_edges // 128)
    tiles = -(-(nodes + 1) // 128)
    per_tile = -(-chunks // tiles)
    experts, _, f = a["L0_ffn_w1"].shape
    x = np.zeros((tiles * 128, d), np.float32)
    x[:nodes] = a["x"]
    edges = np.empty((2, tiles * per_tile * 128), np.int32)
    edges[0, n_edges:], edges[1, n_edges:] = 0, nodes
    edges[0, :n_edges], edges[1, :n_edges] = a["src"], a["dst"]
    edges = edges.reshape(2, -1, 128)
    src_t, dst_t = edges[0].T, edges[1].T
    edges = edges[:, :chunks].transpose(1, 0, 2)
    arrays = {
        "x": x, "src_t": src_t, "dst_t": dst_t,
        "edges": edges.reshape(chunks, 256),
        "heads": edges[:, 1, 0].reshape(1, chunks),
        "w_l": a["L0_gnn_W_l"].T, "w_r": a["L0_gnn_W_r"].T, "b_l": a["L0_gnn_b_l"].reshape(1, d),
        "gamma1": a["L0_gnn_ln_gamma"].reshape(1, d), "beta1": a["L0_gnn_ln_beta"].reshape(1, d),
        "gate_w": a["L0_ffn_gate_w"], "gate_b": a["L0_ffn_gate_b"].reshape(1, experts),
        "w1": a["L0_ffn_w1"], "b1": a["L0_ffn_b1"].reshape(experts, f // 128, 128).transpose(2, 0, 1).reshape(128, -1),
        "w2": a["L0_ffn_w2"], "b2": a["L0_ffn_b2"].reshape(1, experts * d),
        "gamma2": a["L0_ffn_gamma"].reshape(1, d), "beta2": a["L0_ffn_beta"].reshape(1, d),
    }
    nc = bacc.Bacc("TRN2", target_bir_lowering=False, num_devices=1)
    arrays = {f"in_{name}": np.ascontiguousarray(v) for name, v in arrays.items()}
    args = [nc.dram_tensor(name, v.shape, mybir.dt.from_np(v.dtype), kind="ExternalInput").ap() for name, v in arrays.items()]
    out = nc.dram_tensor("out", (nodes, d), F32, kind="ExternalOutput").ap()
    build(nc, *args, out)
    r = run_bass_kernel_spmd(nc, [arrays], core_ids=[0])
    return r.results[0]["out"]
```

```python
from contextlib import ExitStack

import concourse.bass as bass
from concourse import mybir

F32 = mybir.dt.float32
I32 = mybir.dt.int32
ALU = mybir.AluOpType
ACT = mybir.ActivationFunctionType
AX = mybir.AxisListType

P = 128
EPS = 1e-5


class Tile:

    def __init__(self, i, c, unroll):
        self.i, self.c, self.unroll = i, c, unroll
        self.slot = c % 2
        self.n = unroll * i + c if isinstance(i, int) else i * unroll + c

    def __add__(self, k):
        return Tile(self.i, self.c + k, self.unroll)

    def inside(self, total):
        return not isinstance(self.i, int) or 0 <= self.n < total

    def slot_of(self, slots):
        return self.c % slots

    def uses(self, slots):
        assert self.unroll % slots == 0
        return self.i * (self.unroll // slots) + self.c // slots + 1


def pipelined(eng, total, before, after, step, unroll=2):
    first = -(-after // unroll) * unroll
    rounds = (total - before - first) // unroll
    for n in range(-before, first):
        step(Tile(0, n, unroll))
    with eng.Fori(0, rounds) as i:
        for c in range(unroll):
            step(Tile(i, first + c, unroll))
    for n in range(first + unroll * rounds, total + after):
        step(Tile(0, n, unroll))


def build(nc, x, src_t, dst_t, edges, heads, w_l, w_r, b_l, gamma1, beta1, gate_w, gate_b, w1, b1, w2, b2,
          gamma2, beta2, out):
    NODES, D = out.shape
    T = x.shape[0] // P
    CHUNKS = edges.shape[0]
    E, _, F = w1.shape
    KD, KF = D // P, F // P
    CPT = src_t.shape[1] // T
    MARGIN = 6
    RING, OHS = 11, 15
    PER_TILE = CPT + 2 * MARGIN
    assert CPT % RING == 0 and PER_TILE % OHS == 0 and 2 * MARGIN < CPT and T * CPT >= CHUNKS
    parts = [[k for k in (-1, 0, 1) if k == 0 or (k == -1 and j < MARGIN) or (k == 1 and j >= CPT - MARGIN)]
             for j in range(CPT)]
    ends = [sum(len(p) for p in parts[:j + 1]) for j in range(CPT)]
    NI = -(-(CHUNKS + T - 1) // P) * P
    IC = NI // P
    B = 7
    NB = T // B
    assert T == B * NB and T % 2 == 1
    JPB = 3
    G0 = T // 2 + 1
    GROUPS = ((0, G0), (G0, T))
    JOBS = [-(-(2 * (b - a) * P + E * (P - 1)) // P) for a, b in GROUPS]
    JOB0 = (0, JOBS[0])
    MT = sum(JOBS)
    WITH_JOBS = T - JOBS[0] // JPB
    assert JOBS[0] == JPB * (T - WITH_JOBS) and WITH_JOBS % 2 == 1 and WITH_JOBS > G0 and JOBS[0] % 6 == 0
    LS, US = 3, 6
    LOOPED = G0 // US
    assert all(j > 6 + 12 * LOOPED for j in JOBS)
    DA = D + 1
    RS = D + 4

    xn_d = nc.dram_tensor("xn_d", [T * P, D], F32).ap()
    x1_d = nc.dram_tensor("x1_d", [T * P, D], F32).ap()
    xs_d = [nc.dram_tensor(f"xs{g}_d", [JOBS[g] * P, D], F32).ap() for g in range(2)]
    ys_d = [nc.dram_tensor(f"ys{g}_d", [JOBS[g] * P, D], F32).ap() for g in range(2)]
    tt_d = nc.dram_tensor("tt_d", [IC, P], I32).ap()

    with ExitStack() as ctx:
        def sb(name, cols, dt=F32):
            return ctx.enter_context(nc.sbuf_tensor(name, [P, cols], dt))

        def sem(name):
            return ctx.enter_context(nc.semaphore(name))

        bank = [ctx.enter_context(nc.psum_tensor(f"bank{i}", [P, 512], F32)) for i in range(8)]

        XN = T * D
        WORK = 30810 + 3 * D
        big = sb("big", XN + WORK)
        xn2_all = big[:, 0:XN]
        cursor = [0]

        def part(base, cols):
            at = base + cursor[0]
            cursor[0] += cols
            assert base + cursor[0] <= (XN + WORK if base else XN)
            return big[:, at:at + cols]

        xn = xn2_all
        cursor[0] = 0
        rows = part(XN, RING * RS)
        onehot = part(XN, OHS * P)
        src_all = part(XN, T * CPT).bitcast(I32)
        rel_all = part(XN, T * CPT)
        w2_base = cursor[0]
        dst_i = part(XN, T * CPT).bitcast(I32)
        first_node = part(XN, T * CPT)
        inside_ = part(XN, T * CPT)
        stats = part(XN, T * 6)
        st = {n: part(XN, T) for n in ("sum", "dif", "var", "std", "mean", "rstd", "nmr")}
        cursor[0] = w2_base
        w2_sb = part(XN, E * KF * D)
        job_base = cursor[0]
        w1_s = [part(XN, KD * F) for _ in range(LS)]
        b2_s = [part(XN, D) for _ in range(2 * LS)]
        xs_s = [part(XN, D) for _ in range(LS)]
        xs_t = part(XN, D)
        h_t = [part(XN, F) for _ in range(2)]
        y_s = [part(XN, D) for _ in range(2)]
        TE = G0 * E
        cursor[0] = job_base
        eq, cand, oh1, oh2, lg2, both, cum, tot, inc, pos_all, prod = [part(XN, TE) for _ in range(11)]
        cmp_ = part(XN, max(JOBS) * E)
        cursor[0] = 0
        d_y1, d_y2, d_o, d_x1 = [part(XN, US * D) for _ in range(4)]
        cursor[0] = 0
        acc = part(XN, T * DA)
        tile_of_item = part(XN, NI).bitcast(I32)
        item_src = part(XN, NI).bitcast(I32)
        item_dst = part(XN, NI + 8)
        cursor[0] = 0
        pairs_i = part(0, IC * 2 * P).bitcast(I32)
        pairs_f = part(0, IC * 2 * P)
        starts = part(0, CHUNKS)
        head_i = pairs_f[:, 0:CHUNKS].bitcast(I32)
        chunk_no = pairs_f[:, CHUNKS:2 * CHUNKS]
        junk = pairs_f[:, 0:CHUNKS]
        cursor[0] = 0
        rows_g = part(0, 16 * RS)
        onehot_g = part(0, 16 * P)

        wl_sb = sb("wl_sb", KD * D)
        wr_sb = sb("wr_sb", KD * D)
        bl_sb = sb("bl_sb", D)
        g1_sb = sb("g1_sb", D)
        be1_sb = sb("be1_sb", D)
        gw_sb = sb("gw_sb", KD * E)
        gb_sb = sb("gb_sb", E)
        logits = sb("logits", T * E)
        nx, nxn, agg_s, f_s, s_s, x1_s, xn2_s, xn2_t = [sb(f"node_{n}", D) for n in ("x", "xn", "agg", "f", "s", "x1", "xn2", "xn2_t")]
        x1b_s = sb("node_x1b", D)
        b1_sb = sb("b1_sb", E * KF)
        aggx_t = sb("node_aggx_t", 2 * D)
        deg_s, nstat, nmv, nvar, nstd, nrstd = sb("deg_s", 1), sb("nstat", 6), sb("nmv", 2), sb("nvar", 1), sb("nstd", 1), sb("nrstd", 1)
        src_now = sb("src_now", 2 * CPT, I32)
        rel_now = sb("rel_now", 2 * CPT)
        flag_f, flag_i = sb("flag_f", 1), sb("flag_i", 1, I32)
        iota3 = sb("iota3", 3 * P)
        d_stat, d_mv, d_var, d_std, d_rstd = [sb(f"d_{n}", US * w) for n, w in
                                              (("stat", 6), ("mv", 2), ("var", 1), ("std", 1), ("rstd", 1))]

        ident = sb("ident", P)
        below = sb("below", P)
        ones = sb("ones", P)
        zeros = sb("zeros", D)
        g2_sb = sb("g2_sb", D)
        be2_sb = sb("be2_sb", D)
        item_no = sb("item_no", IC)
        item_c = sb("item_c", IC)
        item_ci = sb("item_ci", IC, I32)
        item_t = sb("item_t", IC)
        item_nt = sb("item_nt", IC)
        item_tc = sb("item_tc", IC)
        item_ti = sb("item_ti", P, I32)
        src_stage = sb("src_stage", 16, I32)
        e_no = sb("e_no", E)
        m_no = sb("m_no", max(JOBS))
        v1, v2, i1, i2, p1, p2, ed = [sb(n, T) for n in ("v1", "v2", "i1", "i2", "p1", "p2", "ed")]
        posf = sb("posf", 2 * T)
        pos_i = sb("pos_i", 2 * T, I32)
        nt_i = sb("nt_i", E, I32)
        nt_f = sb("nt_f", E)
        end_f = sb("end_f", E)
        base_f = sb("base_f", E)
        et_f = sb("et_f", max(JOBS))
        et_i = sb("et_i", MT, I32)

        turns = sem("turns")
        stage = [sem(f"stage{i}_done") for i in range(7)]
        heads_in, params_in, late_in = sem("heads_in"), sem("params_in"), sem("late_in")
        x_in = [sem(f"x_in{i}") for i in range(NB)]
        chunkno_ready, consts_ready, masks_ready, acc_zero = sem("chunkno_ready"), sem("consts_ready"), sem("masks_ready"), sem("acc_zero")
        chunk_ready, nt_ready = sem("chunk_ready"), sem("nt_ready")
        pairs_in, pairs_ready, tables_t = sem("pairs_in"), sem("pairs_ready"), sem("tables_t")
        tc_ready, ti_ready, ti_out, ti_in = sem("tc_ready"), sem("ti_ready"), sem("ti_out"), sem("ti_in")
        var_ready, std_ready, norm_ready = sem("var_ready"), sem("std_ready"), sem("norm_ready")
        xn_even, xn_odd, xn_out = sem("xn_even"), sem("xn_odd"), sem("xn_out")
        idx_ready, oh_ready, mm_done, acc_done = sem("idx_ready"), sem("oh_ready"), sem("mm_done"), sem("acc_done")
        rows_in = [sem(f"rows_in{k}") for k in range(16)]
        xs0_out = sem("xs0_out")
        tables_in, ok_ready, ok_summed = sem("tables_in"), sem("ok_ready"), sem("ok_summed")
        now_ready, ohe_ready, mme_done = sem("now_ready"), sem("ohe_ready"), sem("mme_done")
        rowse_in = [sem(f"rowse_in{k}") for k in range(RING)]
        node_in, s_ready, agg_ready, nt_done, ntt_ready = sem("node_in"), sem("s_ready"), sem("agg_ready"), sem("nt_done"), sem("ntt_ready")
        f_done, gelu_done, var1_ready, std1_ready, var2_ready, std2_ready = [sem(n) for n in (
            "f_done", "gelu_done", "var1_ready", "std1_ready", "var2_ready", "std2_ready")]
        x1b_ready, x1b_out, w2_in, d_x1_in = [sem(n) for n in ("x1b_ready", "x1b_out", "w2_in", "d_x1_in")]
        xn2_ready, xn2_kept, xn2t_done, xn2t_ready, lg_done, lg_ready = [sem(n) for n in (
            "xn2_ready", "xn2_kept", "xn2t_done", "xn2t_ready", "lg_done", "lg_ready")]
        diff_ready, exp_ready, both_ready, counts_done = sem("diff_ready"), sem("exp_ready"), sem("both_ready"), sem("counts_done")
        routed, sc_out = sem("routed"), sem("sc_out")
        job_in = [sem(f"job_in{k}") for k in range(LS)]
        y_out = [sem(f"y_out{k}") for k in range(2)]
        xt_done, xst_ready, h_done, ht_ready, y_done, y_ready = [sem(n) for n in (
            "xt_done", "xst_ready", "h_done", "ht_ready", "y_done", "y_ready")]
        dy_in = [sem(f"dy_in{k}") for k in range(US)]
        dy_used, dvar_ready, dstd_ready, do_ready, d_out = [sem(n) for n in ("dy_used", "dvar_ready", "dstd_ready", "do_ready", "d_out")]

        EVEN = (B + 1) // 2

        block = ctx.enter_context(nc.Block())

        def is_even(eng):
            return eng.If(eng.value_load(flag_i[0:1, 0:1], min_val=0, max_val=P) >= P)

        def turn(eng, s, value):
            if isinstance(value, int):
                if value > 0:
                    eng.wait_ge(s, value)
            else:
                eng.wait_ge(s, value)
                eng.sem_inc(turns, 1)

        def stage_end(eng, k):
            eng.drain().then_inc(stage[k], 1)
            eng.wait_ge(stage[k], 5)

        def cols(t, n, width):
            return t[:, bass.ds(n * width, width)] if not isinstance(n, int) else t[:, n * width:(n + 1) * width]

        def rows3(t, n):
            r = t[bass.ds(n * (B * P), B * P), :] if not isinstance(n, int) else t[n * B * P:(n + 1) * B * P, :]
            return r.rearrange("(t p) d -> p t d", p=P)

        def by_tile(a):
            return a.rearrange("p (t d) -> p t d", d=D)

        def dram_rows(t, n, count=P):
            return t[bass.ds(n * P, count), :] if not isinstance(n, int) else t[n * P:n * P + count, :]

        def expert_of(eng, job):
            return eng.value_load(et_i[0:1, bass.ds(job.n, 1)] if not isinstance(job.n, int) else et_i[0:1, job.n:job.n + 1],
                                  min_val=0, max_val=E - 1)

        def dense_jobs(g, eng, step, others=None):
            start, end = JOB0[g], JOB0[g] + JOBS[g]
            for c in range(start, start + 6):
                step(Tile(0, c, 12), c == start, False)
            with eng.Fori(0, LOOPED) as i:
                for c in range(12):
                    step(Tile(i, start + 6 + c, 12), False, False)
                    if others:
                        others(i, c)
            for c in range(start + 6 + 12 * LOOPED, end):
                step(Tile(0, c, 12), False, c == end - 1)

        @block.sync
        def _(sp):
            sp.dma_start(dst_i, dst_t).then_inc(heads_in, 16)
            for c in range(NB):
                sp.dma_start(by_tile(cols(xn, c, B * D)), rows3(x, c)).then_inc(x_in[c], 16)
            sp.dma_start(src_all, src_t).then_inc(tables_in, 16)
            for dst, src in ((g2_sb, gamma2), (be2_sb, beta2), (g1_sb, gamma1), (be1_sb, beta1)):
                sp.dma_start(dst[:, :], src.to_broadcast([P, D])).then_inc(params_in, 16)
            sp.dma_start(bl_sb[0:1, :], b_l).then_inc(params_in, 16)
            sp.dma_start(gb_sb[0:1, :], gate_b).then_inc(params_in, 16)
            for dst, src in ((wl_sb, w_l), (wr_sb, w_r), (gw_sb, gate_w)):
                sp.dma_start(dst[:, :].rearrange("p (k n) -> p k n", k=KD), src.rearrange("(k p) n -> p k n", p=P)).then_inc(params_in, 16)
            for c in range(NB):
                sp.wait_ge(xn_even, EVEN * (c + 1))
                sp.wait_ge(xn_odd, (B - EVEN) * (c + 1))
                sp.dma_start(rows3(xn_d, c), by_tile(cols(xn, c, B * D))).then_inc(xn_out, 16)
            sp.wait_ge(xn_out, 16 * NB)
            sp.wait_ge(tables_in, 16)
            sp.wait_ge(params_in, 16 * 9)
            stage_end(sp, 0)

            sp.dma_start(b1_sb[:, :], b1).then_inc(w2_in, 16)

            def w2_load(e):
                sp.dma_start(w2_sb.rearrange("p (e k h) -> p e k h", e=E, k=KF)[:, bass.ds(e, 1)],
                             w2[bass.ds(e, 1)].rearrange("e (k p) h -> p e k h", p=P)).then_inc(w2_in, 16)

            ZEROS = (JPB, JOBS[1] // E)
            SHARES = [JOBS[g] // ZEROS[g] for g in range(2)]
            assert SHARES[1] == E <= SHARES[0] < WITH_JOBS - 1 and all(JOBS[g] % ZEROS[g] == 0 for g in range(2))

            def xs_zero(g, n):
                r = ZEROS[g] * P
                sp.dma_start(xs_d[g][bass.ds(n * r, r), :].rearrange("(p m) d -> p m d", p=P),
                             zeros[:, :].rearrange("p (a d) -> p a d", a=1).to_broadcast([P, ZEROS[g], D])).then_inc(xs0_out, 16)

            def node_load(n):
                turn(sp, nt_done, n)
                turn(sp, s_ready, n)
                sp.dma_start(nxn[:, :], dram_rows(xn_d, n)).then_inc(node_in, 16)
                sp.dma_start(nx[:, :], dram_rows(x, n)).then_inc(node_in, 16)

            def job_load(g, job):
                k = job.slot_of(LS)
                e = expert_of(sp, job)
                sp.dma_start(xs_s[k], dram_rows(xs_d[g], (job + -JOB0[g]).n)).then_inc(job_in[k], 16)
                sp.dma_start(b2_s[job.slot_of(2 * LS)], b2[bass.ds(e, 1), :].to_broadcast([P, D])).then_inc(job_in[k], 16)
                sp.dma_start(w1_s[k].rearrange("p (a k f) -> p a k f", a=1, k=KD),
                             w1[bass.ds(e, 1)].rearrange("e (k p) f -> p e k f", p=P)).then_inc(job_in[k], 16)

            def next_load(g, job):
                if (job + LS).inside(JOB0[g] + JOBS[g]):
                    turn(sp, h_done, job.n + 1)
                    job_load(g, job + LS)

            def result_store(g, job):
                turn(sp, y_ready, job.n + 2)
                sp.dma_start(dram_rows(ys_d[g], (job + -JOB0[g]).n), y_s[job.slot]).then_inc(y_out[job.slot], 16)

            def dense_step(g, job):
                next_load(g, job + 1)
                result_store(g, job)

            def x1_store(n):
                turn(sp, x1b_ready, n + 1)
                sp.dma_start(dram_rows(x1_d, n), x1b_s[:, :]).then_inc(x1b_out, 16)

            def jobs_start(g):
                sp.wait_ge(routed, g + 1)
                a, b = GROUPS[g]
                sp.wait_ge(sc_out, 32 * b)
                for c in range(LS):
                    job_load(g, Tile(0, JOB0[g] + c, 12))
                next_load(g, Tile(0, JOB0[g], 12))

            with is_even(sp):
                sp.dma_start(nxn[:, :], dram_rows(xn_d, 0)).then_inc(node_in, 16)
                sp.dma_start(nx[:, :], dram_rows(x, 0)).then_inc(node_in, 16)
                x1_store(0)
                with sp.Fori(1, 1 + E) as n:
                    node_load(n)
                    xs_zero(0, n - 1)
                    xs_zero(1, n - 1)
                    w2_load(n - 1)
                    x1_store(n)
                with sp.Fori(1 + E, 1 + SHARES[0]) as n:
                    node_load(n)
                    xs_zero(0, n - 1)
                    x1_store(n)
                with sp.Fori(1 + SHARES[0], WITH_JOBS - 1) as n:
                    node_load(n)
                    x1_store(n)
                node_load(WITH_JOBS - 1)
                jobs_start(0)

                def job_step(job):
                    result_store(0, job)
                    next_load(0, job + 1)

                def tile_step(t, jobs):
                    job_step(jobs[0])
                    node_load(t.n)
                    job_step(jobs[1])
                    job_step(jobs[2])
                    x1_store(t.n - 1)

                with sp.Fori(0, (T - WITH_JOBS) // 2 - 1) as i:
                    for c in range(2):
                        tile_step(Tile(i, WITH_JOBS + c, 2), [Tile(i, JPB * c + k, 2 * JPB) for k in range(JPB)])
                for c in range(2):
                    tile_step(Tile(0, T - 2 + c, 2), [Tile(0, JOBS[0] - (2 - c) * JPB + k, 2 * JPB) for k in range(JPB)])
                x1_store(T - 1)
            with sp.Else():
                sp.dma_start(head_i, heads.to_broadcast([P, CHUNKS])).then_inc(heads_in, 16)
                sp.wait_ge(ti_ready, 1)
                sp.dma_start(tt_d, item_ti[0:IC, :]).then_inc(ti_out, 16)
                sp.wait_ge(ti_out, 16)
                sp.dma_start(tile_of_item[0:1, :], tt_d.rearrange("(a j) p -> a (j p)", a=1)).then_inc(ti_in, 16)
                sp.wait_ge(ti_in, 16)
                stage_end(sp, 1)
                stage_end(sp, 2)
                sp.dma_start(nxn[:, :], dram_rows(xn_d, 0)).then_inc(node_in, 16)
                sp.dma_start(nx[:, :], dram_rows(x, 0)).then_inc(node_in, 16)
                x1_store(0)
                with sp.Fori(1, T) as n:
                    node_load(n)
                    x1_store(n)
                stage_end(sp, 3)
                with sp.Fori(0, E) as e:
                    w2_load(e)
                    xs_zero(0, e)
                    xs_zero(1, e)
                with sp.Fori(E, SHARES[0]) as n:
                    xs_zero(0, n)
                jobs_start(0)
                dense_jobs(0, sp, lambda job, first, last: dense_step(0, job))
            for k in range(2):
                sp.wait_ge(y_out[k], 16 * (JOBS[0] // 2 + 1))
            sp.wait_ge(x1b_out, 16 * (T + 1))
            stage_end(sp, 4)

            jobs_start(1)

            def x1_load(block):
                sp.dma_start(by_tile(d_x1), x1_d[bass.ds(block * (US * P), US * P), :].rearrange("(t p) d -> p t d", p=P)).then_inc(d_x1_in, 16)

            x1_load(0)

            def result_out(block, c):
                if c == 11:
                    turn(sp, do_ready, block + 1)
                    x1_load(block + 1)
                    sp.dma_start(out[bass.ds(block * (US * P), US * P), :].rearrange("(t p) d -> p t d", p=P), by_tile(d_o)).then_inc(d_out, 16)

            dense_jobs(1, sp, lambda job, first, last: dense_step(1, job), result_out)
            for k in range(2):
                sp.wait_ge(y_out[k], 16 * ((MT + 1 - k) // 2 + 1))
            stage_end(sp, 5)

            with sp.Fori(LOOPED, T // US - 1) as block:
                turn(sp, do_ready, block + 1)
                x1_load(block + 1)
                sp.dma_start(out[bass.ds(block * (US * P), US * P), :].rearrange("(t p) d -> p t d", p=P), by_tile(d_o)).then_inc(d_out, 16)
            last = T // US
            sp.wait_ge(do_ready, last)
            sp.dma_start(d_x1[:, 0:D], x1_d[(T - 1) * P:T * P, :]).then_inc(d_x1_in, 16)
            sp.dma_start(out[(last - 1) * US * P:last * US * P, :].rearrange("(t p) d -> p t d", p=P), by_tile(d_o)).then_inc(d_out, 16)
            sp.wait_ge(do_ready, T // US + 1)
            sp.dma_start(out[(T - 1) * P:NODES, :], d_o[0:NODES - (T - 1) * P, 0:D]).then_inc(d_out, 16)
            sp.wait_ge(d_out, 16 * (T // US + 2))
            stage_end(sp, 6)

        @block.gpsimd
        def _(pool):
            def count_up(t, pattern, base=0, channel_multiplier=0):
                return pool.iota(t, pattern=pattern, base=base, channel_multiplier=channel_multiplier, allow_small_or_imprecise_dtypes=True)

            count_up(first_node, [[P, T], [0, CPT]]).then_inc(consts_ready, 1)
            count_up(item_no[:, :], [[P, IC]], channel_multiplier=1).then_inc(consts_ready, 1)
            count_up(iota3[:, :], [[1, 3 * P]], base=-P).then_inc(consts_ready, 1)
            count_up(e_no[:, :], [[1, E]]).then_inc(consts_ready, 1)
            count_up(m_no[:, :], [[1, max(JOBS)]]).then_inc(consts_ready, 1)
            pool.memset(ident[:, :], 0.0).then_inc(consts_ready, 1)
            pool.memset(below[:, :], 1.0).then_inc(consts_ready, 1)
            pool.memset(ones[:, :], 1.0).then_inc(consts_ready, 1)
            pool.memset(zeros[:, :], 0.0).then_inc(consts_ready, 1)
            pool.wait_ge(consts_ready, 9)
            pool.affine_select(out=ident[:, :], in_=ident[:, :], compare_op=ALU.not_equal, fill=1.0, base=0,
                               pattern=[[-1, P]], channel_multiplier=1).then_inc(masks_ready, 1)
            pool.affine_select(out=below[:, :], in_=below[:, :], compare_op=ALU.is_gt, fill=0.0, base=0,
                               pattern=[[1, P]], channel_multiplier=-1).then_inc(masks_ready, 1)
            stage_end(pool, 0)

            def gather_tile(t):
                turn(pool, now_ready, 2 * t.n + 2)
                for j in range(CPT):
                    turn(pool, mme_done, t.n * PER_TILE + (ends[j - RING] if j >= RING else ends[j - RING + CPT] - PER_TILE))
                    k = j % RING
                    at = t.slot * CPT + j
                    pool.indirect_dma_start(rows[:, k * RS:k * RS + D], None, xn_d,
                                            bass.IndirectOffsetOnAxis(ap=src_now[:, at:at + 1], axis=0)).then_inc(rowse_in[k], 16)

            def scatter(g):
                pool.wait_ge(routed, g + 1)
                pool.wait_ge(xs0_out, 16 * (JOBS[0] // JPB + E))
                for n in range(*GROUPS[g]):
                    for c in range(2):
                        at = 2 * n + c
                        pool.indirect_dma_start(xs_d[g], bass.IndirectOffsetOnAxis(ap=pos_i[:, at:at + 1], axis=0),
                                                xn2_all[:, n * D:(n + 1) * D], None).then_inc(sc_out, 16)

            with is_even(pool):
                gather_tile(Tile(0, 0, 2))
                with pool.Fori(0, (WITH_JOBS - 1) // 2) as i:
                    gather_tile(Tile(i, 1, 2))
                    gather_tile(Tile(i, 2, 2))
                scatter(0)
                with pool.Fori(0, (T - WITH_JOBS) // 2) as i:
                    gather_tile(Tile(i, WITH_JOBS, 2))
                    gather_tile(Tile(i, WITH_JOBS + 1, 2))
            with pool.Else():
                count_up(chunk_no, [[1, CHUNKS]]).then_inc(chunkno_ready, 1)
                pool.memset(acc[:, :], 0.0).then_inc(acc_zero, 1)
                pool.wait_ge(chunk_ready, 1)
                for j in range(IC):
                    pool.indirect_dma_start(pairs_i[:, j * 2 * P:(j + 1) * 2 * P], None, edges,
                                            bass.IndirectOffsetOnAxis(ap=item_ci[:, j:j + 1], axis=0)).then_inc(pairs_in, 16)
                pool.wait_ge(pairs_in, 16 * IC)
                stage_end(pool, 1)
                with pool.Fori(0, NI // 16) as g:
                    for q in range(4):
                        turn(pool, idx_ready, 4 * g + q + 1)
                        for k in range(4 * q, 4 * q + 4):
                            pool.indirect_dma_start(rows_g[:, k * RS:k * RS + D], None, xn_d,
                                                    bass.IndirectOffsetOnAxis(ap=src_stage[:, k:k + 1], axis=0)).then_inc(rows_in[k], 16)
                stage_end(pool, 2)
                stage_end(pool, 3)
                scatter(0)
            stage_end(pool, 4)
            scatter(1)

            for n in range(T):
                if n == G0:
                    stage_end(pool, 5)
                k = n % US
                if n >= US:
                    pool.wait_ge(dy_used, n - US + 1)
                for c, slot in enumerate((d_y1, d_y2)):
                    at = 2 * n + c
                    pool.indirect_dma_start(slot[:, k * D:(k + 1) * D], None, ys_d[n >= G0],
                                            bass.IndirectOffsetOnAxis(ap=pos_i[:, at:at + 1], axis=0)).then_inc(dy_in[k], 16)
            stage_end(pool, 6)

        @block.scalar
        def _(act):
            act.wait_ge(var_ready, 1)
            act.activation(st["std"][:, :], st["var"][:, :], ACT.Sqrt).then_inc(std_ready, 1)
            act.wait_ge(norm_ready, 1)
            with act.Fori(0, NB) as i:
                for k in range(EVEN, B):
                    n = B * i + k
                    act.activation(cols(xn, n, D), cols(xn, n, D), ACT.Identity,
                                   scale=cols(st["rstd"], n, 1), bias=cols(st["nmr"], n, 1)).then_inc(xn_odd, 1)
            stage_end(act, 0)

            def node_act(piece, n):
                if piece == "t":
                    turn(act, nt_done, n + 1)
                    act.activation(aggx_t[:, :], bank[2][:, :], ACT.Copy).then_inc(ntt_ready, 1)
                elif piece == "gelu":
                    turn(act, f_done, n + 1)
                    act.activation(f_s[:, :], bank[3][:, 0:D], ACT.Gelu).then_inc(gelu_done, 1)
                elif piece == "std1":
                    turn(act, var1_ready, n + 1)
                    act.activation(nstd[:, :], nvar[:, :], ACT.Sqrt).then_inc(std1_ready, 1)
                elif piece == "std2":
                    turn(act, var2_ready, n + 1)
                    act.activation(nstd[:, :], nvar[:, :], ACT.Sqrt).then_inc(std2_ready, 1)
                elif piece == "keep":
                    turn(act, xn2_ready, n + 1)
                    act.activation(cols(xn2_all, n, D), xn2_s[:, :], ACT.Copy).then_inc(xn2_kept, 1)

            def job_act(piece, job):
                if piece == "x":
                    turn(act, xt_done, job.n + 1)
                    act.activation(xs_t, bank[5][:, 0:D], ACT.Copy).then_inc(xst_ready, 1)
                elif piece == "relu":
                    e = expert_of(act, job)
                    turn(act, h_done, job.n + 1)
                    for f in range(KF):
                        ins = act.activation(h_t[job.slot][:, f * P:(f + 1) * P], bank[6][:, f * P:(f + 1) * P], ACT.Relu,
                                             bias=b1_sb[:, bass.ds(e * KF + f, 1)])
                    ins.then_inc(ht_ready, 1)

            def route_act(g):
                a, b = GROUPS[g]
                act.wait_ge(diff_ready, g + 1)
                act.activation(ed[:, a:b], v2[:, a:b], ACT.Exp).then_inc(exp_ready, 1)

            NODE_PIECES = ("t", "gelu", "std1", "std2", "keep")
            WITH_JOB_PIECES = (("x", 0), ("relu", 0), ("x", 1), "t", ("relu", 1), "gelu", "std1", ("x", 2), "std2", ("relu", 2), "keep")

            def stage_tile(t):
                turn(act, mme_done, (t.n - 1) * PER_TILE)
                act.activation(src_now[:, t.slot * CPT:(t.slot + 1) * CPT], cols(src_all, t.n, CPT), ACT.Copy).then_inc(now_ready, 1)
                act.activation(rel_now[:, t.slot * CPT:(t.slot + 1) * CPT], cols(rel_all, t.n, CPT), ACT.Copy).then_inc(now_ready, 1)

            with is_even(act):
                stage_tile(Tile(0, 0, 2))
                stage_tile(Tile(0, 1, 2))
                with act.Fori(0, (WITH_JOBS - 1) // 2) as i:
                    for c in (1, 2):
                        t = Tile(i, c, 2)
                        stage_tile(t + 1)
                        for piece in NODE_PIECES:
                            node_act(piece, t.n - 1)
                route_act(0)
                act.wait_ge(routed, 1)
                act.wait_ge(w2_in, 16 * (E + 1))

                def tile_step(t, jobs, stage_next):
                    if stage_next:
                        stage_tile(t + 1)
                    for piece in WITH_JOB_PIECES:
                        if isinstance(piece, str):
                            node_act(piece, t.n - 1)
                        else:
                            job_act(piece[0], jobs[piece[1]])

                with act.Fori(0, (T - WITH_JOBS) // 2 - 1) as i:
                    for c in range(2):
                        tile_step(Tile(i, WITH_JOBS + c, 2), [Tile(i, JPB * c + k, 2 * JPB) for k in range(JPB)], True)
                for c in range(2):
                    tile_step(Tile(0, T - 2 + c, 2), [Tile(0, JOBS[0] - (2 - c) * JPB + k, 2 * JPB) for k in range(JPB)], c == 0)
                for piece in NODE_PIECES:
                    node_act(piece, T - 1)
            with act.Else():
                act.wait_ge(nt_ready, 1)
                act.wait_ge(pairs_in, 16 * IC)
                act.activation(pairs_f.rearrange("p (j c) -> p j c", c=2 * P)[:, :, 0:P],
                               pairs_i.rearrange("p (j c) -> p j c", c=2 * P)[:, :, 0:P], ACT.Copy).then_inc(pairs_ready, 1)
                for j in range(IC):
                    act.activation(pairs_f[:, j * 2 * P + P:(j + 1) * 2 * P], pairs_i[:, j * 2 * P + P:(j + 1) * 2 * P],
                                   ACT.Identity, bias=item_nt[:, j:j + 1]).then_inc(pairs_ready, 1)
                act.wait_ge(tables_t, 2 * IC + 1)
                act.activation(item_ti[0:IC, :], bank[3][0:IC, 2 * P:3 * P], ACT.Copy).then_inc(ti_ready, 1)
                for b in range(0, IC, 4):
                    n = min(4, IC - b) * P
                    act.activation(item_src[:, b * P:b * P + n], bank[b // 4][:, 0:n], ACT.Copy)
                    act.activation(item_dst[:, b * P:b * P + n], bank[4 + b // 4][:, 0:n], ACT.Copy)
                stage_end(act, 1)
                with act.Fori(0, NI // 16) as g:
                    for q in range(4):
                        turn(act, mm_done, 16 * g + 4 * q + 4)
                        act.activation(src_stage[:, 4 * q:4 * q + 4], item_src[:, bass.ds(16 * g + 4 * q, 4)], ACT.Copy).then_inc(idx_ready, 1)
                stage_end(act, 2)
                with act.Fori(0, T) as n:
                    for piece in NODE_PIECES:
                        node_act(piece, n)
                stage_end(act, 3)
                route_act(0)
                act.wait_ge(routed, 1)
                act.wait_ge(w2_in, 16 * (E + 1))
                dense_jobs(0, act, lambda job, first, last: [job_act("x", job), job_act("relu", job)])
            stage_end(act, 4)
            route_act(1)
            act.wait_ge(routed, 2)

            def d_std_of(block, c):
                if c == 7:
                    turn(act, dvar_ready, block + 1)
                    act.activation(d_std[:, :], d_var[:, :], ACT.Sqrt).then_inc(dstd_ready, 1)

            dense_jobs(1, act, lambda job, first, last: [job_act("x", job), job_act("relu", job)], d_std_of)
            stage_end(act, 5)

            with act.Fori(LOOPED, T // US + 1) as block:
                d_std_of(block, 7)
            stage_end(act, 6)

        @block.tensor
        def _(pe):
            pe.wait_ge(masks_ready, 2)
            pe.wait_ge(ok_ready, 1)
            pe.matmul(bank[0][0:1, 0:1], ones[:, 0:1], flag_f[:, :], start=True, stop=True).then_inc(ok_summed, 1)
            pe.sem_inc(xst_ready, 1)
            pe.sem_inc(ht_ready, 1)
            stage_end(pe, 0)

            def node_pe(piece, n):
                if piece == "transpose":
                    turn(pe, agg_ready, n + 1)
                    turn(pe, node_in, 32 * n + 32)
                    for k in range(KD):
                        pe.transpose(bank[2][:, k * P:(k + 1) * P], agg_s[:, k * P:(k + 1) * P], ident[:, :])
                    for k in range(KD):
                        ins = pe.transpose(bank[2][:, D + k * P:D + (k + 1) * P], nxn[:, k * P:(k + 1) * P], ident[:, :])
                    ins.then_inc(nt_done, 1)
                elif piece == "linear":
                    turn(pe, ntt_ready, n + 1)
                    f = bank[3][:, 0:D]
                    for k in range(KD):
                        pe.matmul(f, aggx_t[:, k * P:(k + 1) * P], wl_sb[:, k * D:(k + 1) * D], start=k == 0, stop=False)
                    for k in range(KD):
                        pe.matmul(f, aggx_t[:, D + k * P:D + (k + 1) * P], wr_sb[:, k * D:(k + 1) * D], start=False, stop=False)
                    pe.matmul(f, ones[0:1, :], bl_sb[0:1, :], start=False, stop=True).then_inc(f_done, 1)
                elif piece == "transpose2":
                    turn(pe, xn2_ready, n + 1)
                    for k in range(KD):
                        ins = pe.transpose(bank[4][:, k * P:(k + 1) * P], xn2_s[:, k * P:(k + 1) * P], ident[:, :])
                    ins.then_inc(xn2t_done, 1)
                elif piece == "gate":
                    turn(pe, xn2t_ready, n + 1)
                    g = bank[3][:, D:D + E]
                    for k in range(KD):
                        pe.matmul(g, xn2_t[:, k * P:(k + 1) * P], gw_sb[:, k * E:(k + 1) * E], start=k == 0, stop=False)
                    pe.matmul(g, ones[0:1, :], gb_sb[0:1, :], start=False, stop=True).then_inc(lg_done, 1)

            def job_pe(piece, job):
                k = job.slot_of(LS)
                if piece == "xt":
                    turn(pe, job_in[k], 48 * job.uses(LS))
                    turn(pe, xst_ready, job.n + 1)
                    for d in range(KD):
                        ins = pe.transpose(bank[5][:, d * P:(d + 1) * P], xs_s[k][:, d * P:(d + 1) * P], ident[:, :])
                    ins.then_inc(xt_done, 1)
                elif piece == "h":
                    turn(pe, xst_ready, job.n + 2)
                    turn(pe, ht_ready, job.n + 1)
                    for f in range(KF):
                        for d in range(KD):
                            ins = pe.matmul(bank[6][:, f * P:(f + 1) * P], w1_s[k][:, d * F + f * P:d * F + (f + 1) * P],
                                            xs_t[:, d * P:(d + 1) * P], start=d == 0, stop=d == KD - 1)
                    ins.then_inc(h_done, 1)
                elif piece == "y":
                    e = expert_of(pe, job)
                    turn(pe, ht_ready, job.n + 2)
                    turn(pe, y_ready, job.n + 1)
                    for f in range(KF):
                        ins = pe.matmul(bank[7][:, 0:D], h_t[job.slot][:, f * P:(f + 1) * P],
                                        w2_sb[:, bass.ds(e * (KF * D) + f * D, D)], start=f == 0, stop=f == KF - 1)
                    ins.then_inc(y_done, 1)

            def dense_pe(job, first, last):
                if first:
                    job_pe("xt", job)
                job_pe("h", job)
                if not last:
                    job_pe("xt", job + 1)
                if not first:
                    job_pe("y", job + -1)
                if last:
                    job_pe("y", job)

            def route_pe(g):
                a, b = GROUPS[g]
                pe.wait_ge(both_ready, g + 1)
                for m, mask in enumerate((below, ones)):
                    pe.matmul(bank[5 + m][:, 0:(b - a) * E], mask[:, :], both[:, 0:(b - a) * E], start=True, stop=True).then_inc(counts_done, 1)

            JOB_AT = {0: ("xt", 0), 2: ("h", 0), 5: ("y", 0), 9: ("xt", 1), 12: ("h", 1), 16: ("y", 1), 19: ("xt", 2), 22: ("h", 2), 26: ("y", 2)}
            PE_AT = {10: "transpose", 13: "linear", 24: "transpose2", 28: "gate"}

            def sum_tile(t, first=False, jobs=None):
                for j in range(CPT):
                    if jobs and j in JOB_AT:
                        job_pe(JOB_AT[j][0], jobs[JOB_AT[j][1]])
                    if not first and j in PE_AT:
                        node_pe(PE_AT[j], t.n - 1)
                    turn(pe, ohe_ready, t.n * PER_TILE + ends[j])
                    k = j % RING
                    turn(pe, rowse_in[k], (t.n * (CPT // RING) + j // RING + 1) * 16)
                    for m, side in enumerate(parts[j]):
                        at = (ends[j] - len(parts[j]) + m) % OHS
                        starts_here = (side == 1 and j == CPT - MARGIN) or (first and j == 0)
                        ends_here = side == -1 and j == MARGIN - 1
                        pe.matmul(bank[(t.slot + side) % 2][:, 0:DA], onehot[:, at * P:(at + 1) * P], rows[:, k * RS:k * RS + DA],
                                  start=starts_here, stop=ends_here).then_inc(mme_done, 1)

            with is_even(pe):
                sum_tile(Tile(0, 0, 2), first=True)
                with pe.Fori(0, (WITH_JOBS - 1) // 2) as i:
                    sum_tile(Tile(i, 1, 2))
                    sum_tile(Tile(i, 2, 2))
                route_pe(0)
                pe.wait_ge(routed, 1)
                pe.wait_ge(w2_in, 16 * (E + 1))
                with pe.Fori(0, (T - WITH_JOBS) // 2) as i:
                    for c in range(2):
                        sum_tile(Tile(i, WITH_JOBS + c, 2), jobs=[Tile(i, JPB * c + k, 2 * JPB) for k in range(JPB)])
                for b in range(2):
                    pe.matmul(bank[b][:, 0:DA], zeros[:, 0:P], iota3[:, 0:DA], start=False, stop=True).then_inc(mme_done, 1)
                for piece in PE_AT.values():
                    node_pe(piece, T - 1)
            with pe.Else():
                pe.wait_ge(pairs_ready, 1 + IC)
                for j in range(IC):
                    pe.transpose(bank[j // 4][:, j % 4 * P:(j % 4 + 1) * P], pairs_f[:, j * 2 * P:j * 2 * P + P], ident[:, :]).then_inc(tables_t, 1)
                    pe.transpose(bank[4 + j // 4][:, j % 4 * P:(j % 4 + 1) * P], pairs_f[:, j * 2 * P + P:(j + 1) * 2 * P], ident[:, :]).then_inc(tables_t, 1)
                pe.wait_ge(tc_ready, 1)
                assert 12 < IC <= 14
                pe.transpose(bank[3][0:IC, 2 * P:3 * P], item_tc[:, :], ident[:, :]).then_inc(tables_t, 1)
                stage_end(pe, 1)
                pe.sem_inc(mm_done, 16)
                with pe.Fori(0, NI // 16) as g:
                    for k in range(16):
                        if k % 4 == 0:
                            turn(pe, oh_ready, 16 * g + k + 4)
                            turn(pe, acc_done, 16 * g + k + 4)
                        turn(pe, rows_in[k], 16 * g + 16)
                        pe.matmul(bank[k % 8][:, 0:DA], onehot_g[:, k * P:(k + 1) * P], rows_g[:, k * RS:k * RS + DA],
                                  start=True, stop=True).then_inc(mm_done, 1)
                stage_end(pe, 2)
                with pe.Fori(0, T) as n:
                    for piece in PE_AT.values():
                        node_pe(piece, n)
                stage_end(pe, 3)
                route_pe(0)
                pe.wait_ge(routed, 1)
                pe.wait_ge(w2_in, 16 * (E + 1))
                dense_jobs(0, pe, dense_pe)
            stage_end(pe, 4)
            route_pe(1)
            pe.wait_ge(routed, 2)
            dense_jobs(1, pe, dense_pe)
            stage_end(pe, 5)
            stage_end(pe, 6)

        @block.vector
        def _(dve):
            def then(_):
                dve.drain()

            def var_of(stat, mv, var):
                then(dve.bn_aggr(mv, stat))
                return dve.tensor_scalar(var, mv[:, 1:2], EPS, None, ALU.add)

            dve.wait_ge(consts_ready, 9)
            dve.wait_ge(heads_in, 16)
            then(dve.tensor_tensor(rel_all, dst_i, first_node, ALU.subtract))
            r3, b3, i3 = [a.rearrange("p (t j) -> p t j", j=CPT) for a in (rel_all, first_node, inside_)]
            then(dve.memset(first_node, 0.0))
            then(dve.memset(b3[:, :, 0:MARGIN], -float(P)))
            then(dve.tensor_tensor(inside_, rel_all, first_node, ALU.is_ge))
            then(dve.memset(first_node, float(P)))
            then(dve.memset(b3[:, :, CPT - MARGIN:CPT], 2.0 * P))
            then(dve.tensor_tensor(first_node, rel_all, first_node, ALU.is_lt))
            then(dve.tensor_tensor(inside_, inside_, first_node, ALU.mult))
            dve.tensor_reduce(out=flag_f[:, :], in_=inside_, axis=AX.X, op=ALU.min).then_inc(ok_ready, 1)
            for c in range(NB):
                dve.wait_ge(x_in[c], 16)
                with dve.Fori(0, B) as i:
                    dve.bn_stats(stats[:, bass.ds((i + c * B) * 6, 6)], xn[:, bass.ds((i + c * B) * D, D)])
            s = stats.rearrange("p (t s) -> p s t", s=6)
            dve.drain()
            dve.tensor_tensor(st["sum"][:, :], s[:, 1], s[:, 4], ALU.add)
            dve.tensor_tensor(st["dif"][:, :], s[:, 1], s[:, 4], ALU.subtract)
            then(dve.tensor_tensor(st["var"][:, :], s[:, 2], s[:, 5], ALU.add))
            then(dve.tensor_tensor(st["dif"][:, :], st["dif"][:, :], st["dif"][:, :], ALU.mult))
            then(dve.scalar_tensor_tensor(out=st["var"][:, :], in0=st["dif"][:, :], scalar=D / 4, in1=st["var"][:, :],
                                          op0=ALU.mult, op1=ALU.add))
            dve.tensor_scalar(st["var"][:, :], st["var"][:, :], 1.0 / D, EPS, ALU.mult, ALU.add).then_inc(var_ready, 1)
            dve.tensor_scalar(st["mean"][:, :], st["sum"][:, :], 0.5, None, ALU.mult)
            dve.wait_ge(std_ready, 1)
            then(dve.reciprocal(st["rstd"][:, :], st["std"][:, :]))
            then(dve.scalar_tensor_tensor(out=st["nmr"][:, :], in0=st["mean"][:, :], scalar=-1.0, in1=st["rstd"][:, :],
                                          op0=ALU.mult, op1=ALU.mult).then_inc(norm_ready, 1))
            with dve.Fori(0, NB) as i:
                for k in range(EVEN):
                    n = B * i + k
                    dve.tensor_scalar(cols(xn, n, D), cols(xn, n, D), cols(st["mean"], n, 1), cols(st["rstd"], n, 1),
                                      ALU.subtract, ALU.mult).then_inc(xn_even, 1)
            dve.sem_inc(y_ready, 1)
            for k in range(2):
                dve.sem_inc(y_out[k], 16)
            dve.sem_inc(d_out, 16)
            dve.sem_inc(x1b_out, 16)
            dve.sem_inc(xn2_kept, 1)
            dve.wait_ge(ok_summed, 1)
            then(dve.tensor_copy(flag_i[0:1, :], bank[0][0:1, 0:1]))
            stage_end(dve, 0)

            def node_dve(piece, n, total=None):
                if piece == "s":
                    turn(dve, node_in, 32 * n + 32)
                    then(dve.tensor_tensor(s_s[:, :], nx[:, :], nxn[:, :], ALU.add).then_inc(s_ready, 1))
                    dve.tensor_tensor(s_s[:, :], s_s[:, :], be1_sb[:, :], ALU.add)
                elif piece == "mean":
                    then(dve.tensor_scalar(deg_s[:, :], total[:, D:DA], 1.0, None, ALU.max))
                    then(dve.reciprocal(deg_s[:, :], deg_s[:, :]))
                    dve.tensor_scalar(agg_s[:, :], total[:, 0:D], deg_s[:, :], None, ALU.mult).then_inc(agg_ready, 1)
                elif piece == "stats1":
                    turn(dve, gelu_done, n + 1)
                    then(dve.bn_stats(nstat[:, :], f_s[:, :]))
                    then(var_of(nstat[:, :], nmv[:, :], nvar[:, :]).then_inc(var1_ready, 1))
                elif piece == "x1":
                    turn(dve, std1_ready, n + 1)
                    then(dve.reciprocal(nrstd[:, :], nstd[:, :]))
                    then(dve.tensor_scalar(f_s[:, :], f_s[:, :], nmv[:, 0:1], nrstd[:, :], ALU.subtract, ALU.mult))
                    then(dve.tensor_tensor(f_s[:, :], f_s[:, :], g1_sb[:, :], ALU.mult))
                    then(dve.tensor_tensor(x1_s[:, :], f_s[:, :], s_s[:, :], ALU.add))
                    then(dve.bn_stats(nstat[:, :], x1_s[:, :]))
                    then(var_of(nstat[:, :], nmv[:, :], nvar[:, :]).then_inc(var2_ready, 1))
                elif piece == "xn2":
                    turn(dve, std2_ready, n + 1)
                    turn(dve, xn2_kept, n + 1)
                    then(dve.reciprocal(nrstd[:, :], nstd[:, :]))
                    dve.tensor_scalar(xn2_s[:, :], x1_s[:, :], nmv[:, 0:1], nrstd[:, :], ALU.subtract, ALU.mult).then_inc(xn2_ready, 1)
                    turn(dve, x1b_out, 16 * n + 16)
                    dve.tensor_tensor(x1b_s[:, :], x1_s[:, :], be2_sb[:, :], ALU.add).then_inc(x1b_ready, 1)
                elif piece == "xn2t":
                    turn(dve, xn2t_done, n + 1)
                    dve.tensor_copy(xn2_t[:, :], bank[4][:, 0:D]).then_inc(xn2t_ready, 1)
                elif piece == "logits":
                    turn(dve, lg_done, n + 1)
                    dve.tensor_copy(cols(logits, n, E), bank[3][:, D:D + E]).then_inc(lg_ready, 1)

            DVE_AT = {5: "s", 8: "mean", 17: "stats1", 20: "x1", 23: "xn2", 26: "xn2t", 31: "logits"}
            order = list(DVE_AT.values())

            def job_dve(job):
                turn(dve, y_done, job.n + 1)
                turn(dve, y_out[job.slot], 16 * job.uses(2))
                dve.tensor_tensor(y_s[job.slot], bank[7][:, 0:D], b2_s[job.slot_of(2 * LS)], ALU.add).then_inc(y_ready, 1)

            def route_dve(g):
                a, b = GROUPS[g]
                N = (b - a) * E

                def te(x):
                    return x[:, 0:N].rearrange("p (t e) -> p t e", e=E)

                def over_e(x):
                    return x.rearrange("p (t a) -> p t a", a=1).to_broadcast([P, b - a, E])

                def over_t(x):
                    return x.rearrange("p (a e) -> p a e", a=1).to_broadcast([P, b - a, E])

                for lg, v, i, oh in ((logits[:, a * E:b * E], v1, i1, oh1), (lg2, v2, i2, oh2)):
                    v, i = v[:, a:b], i[:, a:b]
                    then(dve.tensor_reduce(out=v, in_=te(lg), axis=AX.X, op=ALU.max))
                    then(dve.tensor_tensor(te(eq), te(lg), over_e(v), ALU.is_equal))
                    then(dve.scalar_tensor_tensor(out=te(cand), in0=te(eq), scalar=-float(E), in1=over_t(e_no[:, :]), op0=ALU.mult, op1=ALU.add))
                    then(dve.tensor_reduce(out=i, in_=te(cand), axis=AX.X, op=ALU.min))
                    then(dve.tensor_tensor(te(oh), te(cand), over_e(i), ALU.is_equal))
                    if oh is oh1:
                        then(dve.scalar_tensor_tensor(out=lg2[:, 0:N], in0=oh[:, 0:N], scalar=-3.0e38, in1=lg, op0=ALU.mult, op1=ALU.add))
                dve.tensor_tensor(both[:, 0:N], oh1[:, 0:N], oh2[:, 0:N], ALU.add).then_inc(both_ready, 1)
                dve.tensor_tensor(v2[:, a:b], v2[:, a:b], v1[:, a:b], ALU.subtract).then_inc(diff_ready, 1)
                dve.wait_ge(exp_ready, g + 1)
                then(dve.tensor_scalar(p1[:, a:b], ed[:, a:b], 1.0, None, ALU.add))
                then(dve.reciprocal(p1[:, a:b], p1[:, a:b]))
                dve.tensor_tensor(p2[:, a:b], ed[:, a:b], p1[:, a:b], ALU.mult)
                dve.wait_ge(counts_done, 2 * g + 2)
                for m, dst in enumerate((cum, tot)):
                    dve.tensor_copy(dst[:, 0:N], bank[5 + m][:, 0:N])
                dve.drain()
                for e in range(E):
                    dve.tensor_tensor_scan(te(inc)[:, :, e], ones[:, 0:b - a], te(tot)[:, :, e], 0.0, ALU.mult, ALU.add)
                dve.drain()
                then(dve.tensor_scalar(nt_i[:, :], inc[:, N - E:N], float(P - 1), None, ALU.add))
                then(dve.tensor_scalar(nt_i[:, :], nt_i[:, :], 7, None, ALU.arith_shift_right))
                then(dve.tensor_copy(nt_f[:, :], nt_i[:, :]))
                then(dve.tensor_tensor_scan(end_f[:, :], ones[:, 0:E], nt_f[:, :], 0.0, ALU.mult, ALU.add))
                then(dve.tensor_tensor(base_f[:, :], end_f[:, :], nt_f[:, :], ALU.subtract))
                then(dve.tensor_scalar(base_f[:, :], base_f[:, :], float(P), None, ALU.mult))
                then(dve.tensor_tensor(pos_all[:, 0:N], inc[:, 0:N], tot[:, 0:N], ALU.subtract))
                then(dve.tensor_tensor(pos_all[:, 0:N], pos_all[:, 0:N], cum[:, 0:N], ALU.add))
                then(dve.tensor_tensor(te(pos_all), te(pos_all), over_t(base_f[:, :]), ALU.add))
                for c, oh in enumerate((oh1, oh2)):
                    then(dve.tensor_tensor(prod[:, 0:N], oh[:, 0:N], pos_all[:, 0:N], ALU.mult))
                    then(dve.tensor_reduce(out=posf[:, 2 * a:2 * b].rearrange("p (t c) -> p t c", c=2)[:, :, c], in_=te(prod), axis=AX.X, op=ALU.add))
                dve.tensor_copy(pos_i[:, 2 * a:2 * b], posf[:, 2 * a:2 * b])
                M = JOBS[g]
                c3 = cmp_[0:1, 0:M * E].rearrange("p (m e) -> p m e", e=E)
                then(dve.tensor_tensor(c3, end_f[0:1, :].rearrange("p (a e) -> p a e", a=1).to_broadcast([1, M, E]),
                                       m_no[0:1, 0:M].rearrange("p (m a) -> p m a", a=1).to_broadcast([1, M, E]), ALU.is_le))
                then(dve.tensor_reduce(out=et_f[0:1, 0:M], in_=c3, axis=AX.X, op=ALU.add))
                then(dve.tensor_scalar(et_i[0:1, JOB0[g]:JOB0[g] + M], et_f[0:1, 0:M], float(E - 1), None, ALU.min))
                dve.sem_inc(routed, 1)

            JOB_AT = {10: 0, 19: 1, 29: 2}

            def onehots_of(t, first=False, jobs=None):
                turn(dve, now_ready, 2 * t.n + 2)
                for j in range(CPT):
                    if jobs and j in JOB_AT:
                        job_dve(jobs[JOB_AT[j]])
                    if not first and j in DVE_AT:
                        if DVE_AT[j] == "mean":
                            turn(dve, mme_done, t.n * PER_TILE + ends[MARGIN - 1])
                        node_dve(DVE_AT[j], t.n - 1, bank[(t.slot + 1) % 2])
                    turn(dve, mme_done, t.n * PER_TILE + (ends[j] - OHS))
                    for m, side in enumerate(parts[j]):
                        at = (ends[j] - len(parts[j]) + m) % OHS
                        dve.tensor_scalar(onehot[:, at * P:(at + 1) * P], iota3[:, (side + 1) * P:(side + 2) * P],
                                          rel_now[:, t.slot * CPT + j:t.slot * CPT + j + 1], None, ALU.is_equal).then_inc(ohe_ready, 1)

            with is_even(dve):
                then(dve.memset(rows.rearrange("p (k r) -> p k r", r=RS)[:, :, D:D + 1], 1.0))
                onehots_of(Tile(0, 0, 2), first=True)
                with dve.Fori(0, (WITH_JOBS - 1) // 2) as i:
                    onehots_of(Tile(i, 1, 2))
                    onehots_of(Tile(i, 2, 2))
                route_dve(0)
                with dve.Fori(0, (T - WITH_JOBS) // 2) as i:
                    for c in range(2):
                        onehots_of(Tile(i, WITH_JOBS + c, 2), jobs=[Tile(i, JPB * c + k, 2 * JPB) for k in range(JPB)])
                dve.wait_ge(mme_done, T * PER_TILE + 2)
                for piece in order:
                    node_dve(piece, T - 1, bank[(T - 1) % 2])
            with dve.Else():
                dve.wait_ge(heads_in, 32)
                dve.wait_ge(chunkno_ready, 1)
                then(dve.tensor_scalar(head_i, head_i, 7, None, ALU.arith_shift_right))
                then(dve.tensor_tensor(starts, head_i, chunk_no, ALU.add))
                for j in range(IC):
                    then(dve.tensor_scalar(junk[:, 0:CHUNKS - 1], starts[:, 1:CHUNKS], item_no[:, j:j + 1], None, ALU.is_le, ALU.add,
                                           accum_out=item_c[:, j:j + 1]))
                then(dve.tensor_copy(item_ci[:, :], item_c[:, :]).then_inc(chunk_ready, 1))
                then(dve.tensor_tensor(item_t[:, :], item_no[:, :], item_c[:, :], ALU.subtract))
                dve.tensor_scalar(item_nt[:, :], item_t[:, :], -float(P), None, ALU.mult).then_inc(nt_ready, 1)
                dve.tensor_scalar(item_tc[:, :], item_t[:, :], float(T - 1), None, ALU.min).then_inc(tc_ready, 1)
                dve.memset(item_dst[:, NI:NI + 8], -1.0)
                stage_end(dve, 1)

                dve.memset(rows_g.rearrange("p (k r) -> p k r", r=RS)[:, :, D:D + 1], 1.0)
                dve.wait_ge(acc_zero, 1)
                dve.sem_inc(acc_done, 8)
                dve.drain()

                def make_onehots(q, item0):
                    for k in range(4):
                        dst = item_dst[:, bass.ds(item0 + k, 1)] if not isinstance(item0, int) else item_dst[:, item0 + k:item0 + k + 1]
                        s = 4 * q + k
                        dve.tensor_scalar(onehot_g[:, s * P:(s + 1) * P], iota3[:, P:2 * P], dst, None, ALU.is_equal).then_inc(oh_ready, 1)

                def accumulate(q, item0):
                    _, tiles = nc.values_load_multi_w_load_instructions(
                        tile_of_item[0:1, bass.ds(item0, 4)], engines=(mybir.EngineType.DVE,), min_val=0, max_val=T - 1)
                    turn(dve, mm_done, item0 + 20)
                    for k in range(4):
                        a = acc[:, bass.ds(tiles[k] * DA, DA)]
                        dve.tensor_tensor(a, a, bank[4 * (q % 2) + k][:, 0:DA], ALU.add).then_inc(acc_done, 1)
                        dve.drain()

                for q in range(2):
                    make_onehots(q, 4 * q)
                with dve.Fori(0, NI // 16) as g:
                    for q in range(4):
                        make_onehots((q + 2) % 4, 16 * g + 4 * q + 8)
                        accumulate(q, 16 * g + 4 * q)
                stage_end(dve, 2)
                with dve.Fori(0, T) as n:
                    for piece in order:
                        node_dve(piece, n, acc[:, bass.ds(n * DA, DA)])
                stage_end(dve, 3)
                route_dve(0)
                dense_jobs(0, dve, lambda job, first, last: job_dve(job))
            stage_end(dve, 4)
            route_dve(1)

            def combine(block, k):
                n = block * US + k
                o = d_o[:, k * D:(k + 1) * D]
                turn(dve, dy_in[k], (block + 1) * 32)
                if k == 0:
                    turn(dve, d_out, (block + 1) * 16)
                then(dve.scalar_tensor_tensor(out=o, in0=d_y1[:, k * D:(k + 1) * D], scalar=cols(p1, n, 1), in1=cols(xn2_all, n, D), op0=ALU.mult, op1=ALU.add))
                then(dve.scalar_tensor_tensor(out=o, in0=d_y2[:, k * D:(k + 1) * D], scalar=cols(p2, n, 1), in1=o, op0=ALU.mult, op1=ALU.add).then_inc(dy_used, 1))
                dve.bn_stats(d_stat[:, 6 * k:6 * k + 6], o)

            def variances(tiles):
                dve.drain()
                for k in range(tiles):
                    dve.bn_aggr(d_mv[:, 2 * k:2 * k + 2], d_stat[:, 6 * k:6 * k + 6])
                dve.drain()
                dve.tensor_scalar(d_var[:, 0:tiles], d_mv[:, 0:2 * tiles].rearrange("p (b c) -> p b c", c=2)[:, :, 1], EPS, None, ALU.add).then_inc(dvar_ready, 1)

            def deviations(block):
                turn(dve, dstd_ready, block + 1)
                then(dve.reciprocal(d_rstd[:, :], d_std[:, :]))

            def results(block, ks, last):
                for k in ks:
                    o = d_o[:, k * D:(k + 1) * D]
                    dve.scalar_tensor_tensor(out=o, in0=o, scalar=d_mv[:, 2 * k:2 * k + 1], in1=g2_sb[:, :], op0=ALU.subtract, op1=ALU.mult)
                dve.drain()
                turn(dve, d_x1_in, (block + 1) * 16)
                for k in ks:
                    o = d_o[:, k * D:(k + 1) * D]
                    ins = dve.scalar_tensor_tensor(out=o, in0=o, scalar=d_rstd[:, k:k + 1], in1=d_x1[:, k * D:(k + 1) * D], op0=ALU.mult, op1=ALU.add)
                if last:
                    ins.then_inc(do_ready, 1)

            def beside_jobs(block, c):
                if c < US:
                    combine(block, c)
                elif c == US:
                    variances(US)
                elif c == 8:
                    deviations(block)
                    results(block, (0, 1), False)
                elif c == 9:
                    results(block, (2, 3), False)
                elif c == 10:
                    results(block, (4, 5), True)

            dense_jobs(1, dve, lambda job, first, last: job_dve(job), beside_jobs)
            stage_end(dve, 5)

            with dve.Fori(LOOPED, T // US) as block:
                for k in range(US):
                    combine(block, k)
                variances(US)
                deviations(block)
                results(block, range(US), True)
            combine(T // US, 0)
            dve.memset(d_var[:, 1:US], 1.0)
            variances(1)
            deviations(T // US)
            results(T // US, (0,), True)
            stage_end(dve, 6)


def kernel(**inputs):
    import numpy as np
    import concourse.bacc as bacc
    from concourse.bass_utils import run_bass_kernel_spmd

    a = {name: np.asarray(v) for name, v in inputs.items()}
    nodes, d = a["x"].shape
    n_edges = a["src"].shape[0]
    chunks = -(-n_edges // 128)
    tiles = -(-(nodes + 1) // 128)
    per_tile = -(-chunks // tiles)
    experts, _, f = a["L0_ffn_w1"].shape
    x = np.zeros((tiles * 128, d), np.float32)
    x[:nodes] = a["x"]
    edges = np.empty((2, tiles * per_tile * 128), np.int32)
    edges[0, n_edges:], edges[1, n_edges:] = 0, nodes
    edges[0, :n_edges], edges[1, :n_edges] = a["src"], a["dst"]
    edges = edges.reshape(2, -1, 128)
    src_t, dst_t = edges[0].T, edges[1].T
    edges = edges[:, :chunks].transpose(1, 0, 2)
    arrays = {
        "x": x, "src_t": src_t, "dst_t": dst_t,
        "edges": edges.reshape(chunks, 256),
        "heads": edges[:, 1, 0].reshape(1, chunks),
        "w_l": a["L0_gnn_W_l"].T, "w_r": a["L0_gnn_W_r"].T, "b_l": a["L0_gnn_b_l"].reshape(1, d),
        "gamma1": a["L0_gnn_ln_gamma"].reshape(1, d), "beta1": a["L0_gnn_ln_beta"].reshape(1, d),
        "gate_w": a["L0_ffn_gate_w"], "gate_b": a["L0_ffn_gate_b"].reshape(1, experts),
        "w1": a["L0_ffn_w1"], "b1": a["L0_ffn_b1"].reshape(experts, f // 128, 128).transpose(2, 0, 1).reshape(128, -1),
        "w2": a["L0_ffn_w2"], "b2": a["L0_ffn_b2"],
        "gamma2": a["L0_ffn_gamma"].reshape(1, d), "beta2": a["L0_ffn_beta"].reshape(1, d),
    }
    nc = bacc.Bacc("TRN2", target_bir_lowering=False, num_devices=1)
    arrays = {f"in_{name}": np.ascontiguousarray(v) for name, v in arrays.items()}
    args = [nc.dram_tensor(name, v.shape, mybir.dt.from_np(v.dtype), kind="ExternalInput").ap() for name, v in arrays.items()]
    out = nc.dram_tensor("out", (nodes, d), F32, kind="ExternalOutput").ap()
    build(nc, *args, out)
    r = run_bass_kernel_spmd(nc, [arrays], core_ids=[0])
    return r.results[0]["out"]
```
